# Optimizing a Trainium2 kernel written in Bass

```python
import numpy as np
import jax
import jax.numpy as jnp

def _softmax(x, axis=-1):
    return jax.nn.softmax(x, axis=axis)

def _gelu(x):
    return jax.nn.gelu(x, approximate=True)

def _silu(x):
    return jax.nn.silu(x)

def _sigmoid(x):
    return jax.nn.sigmoid(x)

def _layernorm(x, axis=-1, eps=1e-05):
    m = jnp.mean(x, axis=axis, keepdims=True)
    v = jnp.var(x, axis=axis, keepdims=True)
    return (x - m) / jnp.sqrt(v + eps)

def _scatter_add(tgt, idx, src, axis=0):
    return tgt.at[idx].add(src)

def _segment_sum(src, seg, n):
    return jax.ops.segment_sum(src, seg, n)
kernel_name = 'mk_seq_preln_d1_jaxref_r8_724a04'

def setup_inputs(seed: int=0):
    np.random.seed(seed)
    _w = jnp.asarray

    def _L0_attn_setup():
        import jax, jax.numpy as jnp
        import numpy as np
        B, S, D, H = (4, 1024, 128, 16)
        HD = D // H

        def elu_feature_map(x):
            return jax.nn.elu(x) + 1.0
        key = jax.random.key(seed)
        k1, k2, k3 = jax.random.split(key, 3)
        x = jax.random.normal(k1, (B, S, D), dtype=jnp.float32)
        w_qkv = jax.random.normal(k2, (3 * D, D), dtype=jnp.float32) * D ** (-0.5)
        w_out = jax.random.normal(k3, (D, D), dtype=jnp.float32) * D ** (-0.5)
        return {'x': x, 'w_qkv': w_qkv, 'w_out': w_out}
    _L0_attn_in = _L0_attn_setup()

    def _L0_ffn_setup():
        import jax, jax.numpy as jnp
        import numpy as np
        import math
        B, S, H, I, E = (4, 256, 128, 512, 8)
        TOP_K = 2
        CAPACITY_FACTOR = 1.25
        key = jax.random.key(seed)
        k1, k2, k3, k4, k5 = jax.random.split(key, 5)
        x = jax.random.normal(k1, (B, S, H), dtype=jnp.float32)
        W_router = jax.random.normal(k2, (E, H), dtype=jnp.float32) * (1.0 / math.sqrt(H))
        b_router = jnp.zeros((E,), dtype=jnp.float32)
        experts_inter = jax.random.normal(k3, (E, H, I), dtype=jnp.float32) * 0.02
        experts_out = jax.random.normal(k4, (E, I, H), dtype=jnp.float32) * 0.02
        return {'x': x, 'W_router': W_router, 'b_router': b_router, 'experts_inter': experts_inter, 'experts_out': experts_out}
    _L0_ffn_in = _L0_ffn_setup()
    _d = {'L0_attn_x': _L0_attn_in['x'], 'L0_attn_w_qkv': _L0_attn_in['w_qkv'], 'L0_attn_w_out': _L0_attn_in['w_out'], 'L0_ffn_W_router': _L0_ffn_in['W_router'], 'L0_ffn_b_router': _L0_ffn_in['b_router'], 'L0_ffn_experts_inter': _L0_ffn_in['experts_inter'], 'L0_ffn_experts_out': _L0_ffn_in['experts_out']}
    _x0 = _d['L0_attn_x']
    _d['L0_attn_x'] = jax.random.normal(jax.random.fold_in(jax.random.key(seed), 1), (8, 1024, 128), dtype=_x0.dtype)
    del _x0
    return _d

def reference(L0_attn_x, L0_attn_w_qkv, L0_attn_w_out, L0_ffn_W_router, L0_ffn_b_router, L0_ffn_experts_inter, L0_ffn_experts_out):

    def _L0_attn_ref(x, w_qkv, w_out):
        import jax, jax.numpy as jnp
        import numpy as np
        B, S, D, H = (4, 1024, 128, 16)
        HD = D // H

        def elu_feature_map(x):
            return jax.nn.elu(x) + 1.0
        Bv, Sv, Dv = x.shape
        qkv = (x @ w_qkv.T).reshape(Bv, Sv, 3, H, HD)
        qkv = jnp.transpose(qkv, (2, 0, 3, 1, 4))
        q, k, v = (qkv[0], qkv[1], qkv[2])
        q = elu_feature_map(q)
        k = elu_feature_map(k)
        kv = jnp.einsum('bhsd,bhse->bhde', k, v)
        out = jnp.einsum('bhsd,bhde->bhse', q, kv)
        k_sum = k.sum(axis=2)
        normalizer = jnp.einsum('bhsd,bhd->bhs', q, k_sum)[..., None]
        normalizer = jnp.maximum(normalizer, 1e-06)
        out = (out / normalizer).transpose(0, 2, 1, 3).reshape(Bv, Sv, Dv)
        return out @ w_out.T

    def _L0_ffn_ref(x, W_router, b_router, experts_inter, experts_out):
        import jax, jax.numpy as jnp
        import numpy as np
        import math
        B, S, H, I, E = (4, 256, 128, 512, 8)
        TOP_K = 2
        CAPACITY_FACTOR = 1.25
        b, s, h = x.shape
        e = experts_inter.shape[0]
        T = b * s
        capacity = math.ceil(T / e * CAPACITY_FACTOR)
        x_flat = x.reshape(T, h)
        logits = x_flat @ W_router.T + b_router
        weights_flat = jax.nn.softmax(logits, axis=-1)
        top_vals, top_idx = jax.lax.top_k(weights_flat, TOP_K)
        topk_flat = jnp.zeros_like(weights_flat).at[jnp.arange(T)[:, None], top_idx].set(top_vals)
        routing_mask = (topk_flat > 0).astype(jnp.int32)
        order = jnp.argsort(-routing_mask, axis=0, stable=True)
        sorted_mask = jnp.take_along_axis(routing_mask, order, axis=0)
        sorted_mask = sorted_mask[:capacity]
        sorted_idx = order[:capacity]
        used_tokens = (sorted_idx * sorted_mask).reshape(-1)
        mask_flat = sorted_mask.reshape(-1).astype(x.dtype)
        inputs_tokens = x_flat[used_tokens] * mask_flat[:, None]
        inputs_tokens = inputs_tokens.reshape(capacity, e, h)
        inputs_weights = jnp.take_along_axis(topk_flat, sorted_idx, axis=0)
        hmid = jnp.einsum('ceh,ehi->cei', inputs_tokens, experts_inter)
        hmid = jax.nn.relu(hmid)
        out = jnp.einsum('cei,eih->ceh', hmid, experts_out)
        out = out * inputs_weights[:, :, None]
        combined = jnp.zeros((T, h), dtype=x.dtype).at[used_tokens].add(out.reshape(-1, h))
        return combined.reshape(b, s, h)
    x = L0_attn_x
    x = x + _L0_attn_ref(_layernorm(x, axis=-1), L0_attn_w_qkv, L0_attn_w_out)
    x = x + _L0_ffn_ref(_layernorm(x, axis=-1), L0_ffn_W_router, L0_ffn_b_router, L0_ffn_experts_inter, L0_ffn_experts_out)
    return x

_drawn_inputs = setup_inputs


def setup_inputs(seed=0):
    import zlib

    import numpy as np

    out = dict(_drawn_inputs(seed))
    spreads = {'L0_ffn_b_router': (0.0, 0.8)}
    factors = {'L0_ffn_experts_inter': 2.682}
    for name, (base, spread) in spreads.items():
        noise = np.random.default_rng([zlib.crc32(name.encode()), seed]).standard_normal(out[name].shape)
        drawn = base * np.exp(spread * noise) if base else spread * noise
        out[name] = jnp.asarray(drawn.astype(out[name].dtype))
    for name, factor in factors.items():
        out[name] = (out[name] * factor).astype(out[name].dtype)
    return out
```

```python
from contextlib import ExitStack

import concourse.bass as bass
from concourse import mybir

F32 = mybir.dt.float32
BF16 = mybir.dt.bfloat16
I32 = mybir.dt.int32
ALU = mybir.AluOpType
ACT = mybir.ActivationFunctionType
AX = mybir.AxisListType

P = 128
HEADS = 16
TOP = 2
LN_EPS = 1e-5
NORM_MIN = 1e-6
ON_QUEUE = 16
FAR = 16384.0
NO_LOGIT = -3.0e38


class Seq:

    def __init__(self, n, parity, half):
        self.n, self.u, self.half = n, parity, half

    @staticmethod
    def fixed(n):
        return Seq(n, n % 2, n // 2)

    def shift(self, k):
        if isinstance(self.n, int):
            return Seq.fixed(self.n + k)
        v = self.u + k
        return Seq(self.n + k, v % 2, self.half + v // 2)


def wait(eng, sem, value, most=None):
    if isinstance(value, int):
        if most is not None:
            value = min(value, most)
        if value <= 0:
            return
    eng.wait_ge(sem, value)


class Chain:

    def __init__(self, eng, sem, per):
        self.eng, self.sem, self.per = eng, sem, per

    def begin(self, b):
        self.base, self.j = b.n * self.per, 0

    def link(self, ins):
        self.j += 1
        assert self.j <= self.per
        ins.then_inc(self.sem, 1)
        self.eng.wait_ge(self.sem, self.base + self.j)

    def end(self):
        assert self.j == self.per, (self.j, self.per)


def moe_layer(nc, x, w_qkv, w_out, w_router, b_router, w_inter, w_exp_out, out):
    NB, S, D = x.shape
    E, _, I = w_inter.shape
    TILES = S // P
    CH = 2
    TC = TILES // CH
    HD = D // HEADS
    CAP = -(-NB * S * 5 // (E * 4))
    ET = CAP // P
    PAIR = 2
    NCH = ET // PAIR
    IB = I // P
    PAY = D + E + 1
    ON = D + HEADS
    assert D == P and CAP % P == 0 and ET % PAIR == 0 and TC * P == 512

    x_v = x.rearrange("b (p t) d -> b p (t d)", p=P)
    out_v = out.rearrange("b (p t) d -> b p (t d)", p=P)
    out_rows = out.rearrange("b s d -> (b s) d")
    places = nc.dram_tensor("places", [E * CAP, PAY], F32).ap()
    places_v = places.rearrange("(e p t) c -> e p (t c)", e=E, p=P)
    w2_v = w_exp_out.rearrange("e (c p) h -> e p c h", p=P)

    with ExitStack() as ctx:
        def sb(name, shape, dt=F32):
            return ctx.enter_context(nc.sbuf_tensor(name, shape, dt))

        def sem(name):
            return ctx.enter_context(nc.semaphore(name))

        bank = [ctx.enter_context(nc.psum_tensor(f"bank{i}", [P, 512], F32)) for i in range(8)]

        ident = sb("ident", [P, P])
        ident_bf = sb("ident_bf", [P, P], BF16)
        before = sb("before", [P, P], BF16)
        ones_bf = sb("ones_bf", [P, P], BF16)
        head_mask = sb("head_mask", [P, HEADS, HD])
        head_sel = sb("head_sel", [P, HEADS])
        first_e = sb("first_e", [P, TILES, E])
        base_e = sb("base_e", [P, TILES, E])
        bias_e = sb("bias_e", [P, E])
        w_raw = sb("w_raw", [P, 4, P])
        wr_raw = sb("wr_raw", [E, P])
        w_t = sb("w_t", [P, 4, P])
        wr_t = sb("wr_t", [P, E])
        empty = sb("empty", [P, ET, PAY])
        xs = sb("xs", [P, NB, TILES, D])
        st1 = sb("st1", [P, TILES, 6])
        st2 = sb("st2", [P, TILES, 6])
        ln1 = sb("ln1", [P, 10, TILES])
        ln2 = sb("ln2", [P, 10, TILES])
        xn = sb("xn", [P, TILES, D + 1])
        xt = sb("xt", [P, CH, 512])
        kx = sb("kx", [P, CH, 512])
        qx = sb("qx", [P, CH, 512])
        phik = sb("phik", [P, CH, 512])
        phiqt = sb("phiqt", [P, CH, 512])
        g_sb = sb("g_sb", [P, D + 1])
        gt_sb = sb("gt_sb", [P, D])
        kvn = sb("kvn", [P, ON])
        nrm = sb("nrm", [P, CH, TC * HEADS])
        rnrm = sb("rnrm", [P, CH, TC * HEADS])
        on = sb("on", [P, CH, 512])
        ot = sb("ot", [P, CH, 512])
        x1 = sb("x1", [P, TILES, D])
        pay = sb("pay", [P, 2, TILES, PAY])
        x1t = sb("x1t", [P, CH, 512])
        rt = sb("rt", [P, 16, TILES, E])
        rm = sb("rm", [P, 8, TILES])
        mask_bf = sb("mask_bf", [P, TILES, E], BF16)
        seen = sb("seen", [P, E], F32)
        seen_bf = sb("seen_bf", [P, E], BF16)
        choice = sb("choice", [P, TOP, TILES])
        spot = sb("spot", [P, 2, TOP, TILES], I32)
        rows = sb("rows", [P, 2, ET, PAY])
        w1 = sb("w1", [P, 2, I])
        w2 = sb("w2", [P, 2, IB, D])
        rt_t = sb("rt_t", [P, 2, PAIR * P])
        hid = sb("hid", [P, 2, IB, PAIR * P])
        yo = sb("yo", [P, 2, ET, D])

        w_in, wr_in = sem("w_in"), sem("wr_in")
        x_in = [sem(f"x_in{u}") for u in range(2)]
        const_z, const_done, payload_ids = sem("const_z"), sem("const_done"), sem("payload_ids")
        empty_set, empty_stored = sem("empty_set"), sem("empty_stored")
        ones_set = sem("ones_set")
        w_turned, w_kept = sem("w_turned"), sem("w_kept")
        n_chain, var1, ln1_log, root1, xn_ready = (sem(s) for s in ("n_chain", "var1", "ln1_log", "root1", "xn_ready"))
        x_turned = [sem(f"x_turned{c}") for c in range(CH)]
        xt_ready = [sem(f"xt_ready{c}") for c in range(CH)]
        k_made, q_made = sem("k_made"), sem("q_made")
        k_relu, q_relu, k_exp, q_exp = (sem(s) for s in ("k_relu", "q_relu", "k_exp", "q_exp"))
        phik_ready, phiq_ready = sem("phik_ready"), sem("phiq_ready")
        g_half, g_made, g_kept, g_turned, gt_kept, kv_made, kvn_ready = (
            sem(s) for s in ("g_half", "g_made", "g_kept", "g_turned", "gt_kept", "kv_made", "kvn_ready"))
        o_made, o_chain, o_ready = sem("o_made"), sem("o_chain"), sem("o_ready")
        o_turned = [sem(f"o_turned{c}") for c in range(CH)]
        ot_ready = [sem(f"ot_ready{c}") for c in range(CH)]
        y_made, x1_ready, x1_stored = sem("y_made"), sem("x1_ready"), sem("x1_stored")
        b_chain, var2, ln2_log, root2, ln2_ready, pay_x = (
            sem(s) for s in ("b_chain", "var2", "ln2_log", "root2", "ln2_ready", "pay_x"))
        x1_turned = [sem(f"x1_turned{c}") for c in range(CH)]
        x1t_ready = [sem(f"x1t_ready{c}") for c in range(CH)]
        logits_made, logits_kept, c_chain, shifted, exps, mask_ready = (
            sem(s) for s in ("logits_made", "logits_kept", "c_chain", "shifted", "exps", "mask_ready"))
        pool_going = sem("pool_going")
        pos_made, spots_ready = sem("pos_made"), sem("spots_ready")
        sent = [sem(f"sent{u}") for u in range(2)]
        rows_in = [sem(f"rows_in{u}") for u in range(2)]
        w1_in = [sem(f"w1_in{u}") for u in range(2)]
        w2_in = [sem(f"w2_in{u}") for u in range(2)]
        r_turned, rt_ready, h_made, h_act, h_dve, e_made, yo_ready = (
            sem(s) for s in ("r_turned", "rt_ready", "h_made", "h_act", "h_dve", "e_made", "yo_ready"))
        added = [sem(f"added{u}") for u in range(2)]

        b_t0, b_t1, b_k, b_q, b_g, b_o0, b_o1, b_y = bank
        o_bank = [b_o0, b_o1]
        GT0, KV0 = 160, 320
        POS0 = TILES * E

        LOOP = (3, 7)

        def run(eng, step):
            for t in range(-1, LOOP[0]):
                step(Seq.fixed(t) if t >= 0 else None, t)
            with eng.Fori(0, (LOOP[1] - LOOP[0]) // 2) as i:
                for k in range(2):
                    step(Seq(i * 2 + (LOOP[0] + k), (LOOP[0] + k) % 2, i + (LOOP[0] + k) // 2), LOOP[0] + k)
            for t in range(LOOP[1], NB + 2):
                step(Seq.fixed(t), t)

        def stages(b, t):
            def at(k):
                if not 0 <= t - k < NB:
                    return None
                return Seq.fixed(t - k) if b is None else b.shift(-k)
            return at(-1), at(0), at(1), at(2)

        def run_pairs(eng, pair):
            pair([Seq.fixed(0), Seq.fixed(1)])
            with eng.Fori(1, E // 2) as i:
                pair([Seq(i * 2, 0, i), Seq(i * 2 + 1, 1, i)])

        def run_experts(eng, expert):
            run_pairs(eng, lambda pair: [expert(e) for e in pair])

        block = ctx.enter_context(nc.Block())

        @block.sync
        def _(sp):
            def load_x(b):
                wait(sp, x_in[b.u], b.half * ON_QUEUE)
                sp.dma_start(xs[:, b.n].rearrange("p t d -> p (t d)"), x_v[b.n]).then_inc(x_in[b.u], ON_QUEUE)

            load_x(Seq.fixed(0))
            sp.dma_start(w_raw[:, 0:3, :], w_qkv.rearrange("(c p) d -> p c d", p=P)).then_inc(w_in, ON_QUEUE)
            sp.dma_start(w_raw[:, 3, :], w_out).then_inc(w_in, ON_QUEUE)
            sp.dma_start(wr_raw[:], w_router).then_inc(w_in, ON_QUEUE)
            sp.dma_start(bias_e[:], b_router.rearrange("(a e) -> a e", a=1).to_broadcast([P, E])).then_inc(wr_in, ON_QUEUE)
            load_x(Seq.fixed(1))
            sp.wait_ge(empty_set, 2)
            for e in range(E):
                sp.dma_start(places_v[e], empty[:].rearrange("p t c -> p (t c)")).then_inc(empty_stored, ON_QUEUE)
            with sp.Fori(1, NB // 2) as i:
                for u in range(2):
                    load_x(Seq(i * 2 + u, u, i))

            def load_expert(e):
                wait(sp, e_made, (e.half - 1) * 2 * NCH + (e.u + 1) * NCH)
                wait(sp, added[e.u], e.half * ET * ON_QUEUE)
                sp.dma_start(rows[:, e.u].rearrange("p t c -> p (t c)"), places_v[e.n]).then_inc(rows_in[e.u], ON_QUEUE)
                sp.dma_start(w1[:, e.u], w_inter[e.n]).then_inc(w1_in[e.u], ON_QUEUE)
                sp.dma_start(w2[:, e.u], w2_v[e.n]).then_inc(w2_in[e.u], ON_QUEUE)

            def store_x1(b):
                sp.wait_ge(x1_ready, b.n * CH + CH)
                sp.dma_start(out_v[b.n], x1[:].rearrange("p t d -> p (t d)")).then_inc(x1_stored, ON_QUEUE)

            with sp.Fori(0, NB) as b:
                store_x1(Seq(b, 0, 0))
            for u in range(2):
                sp.wait_ge(sent[u], NB // 2 * TILES * TOP * ON_QUEUE)
            for u in range(2):
                load_expert(Seq.fixed(u))
            with sp.Fori(1, E // 2) as i:
                for u in range(2):
                    load_expert(Seq(i * 2 + u, u, i))

        @block.gpsimd
        def _(pool):
            g = nc.gpsimd
            g.memset(ident[:], 0.0).then_inc(const_z, 1)
            g.memset(before[:], 1.0).then_inc(const_z, 1)
            g.memset(head_mask[:], 1.0).then_inc(const_z, 1)
            g.memset(head_sel[:], 1.0).then_inc(const_z, 1)
            g.memset(ones_bf[:], 1.0).then_inc(const_done, 1)
            pool.wait_ge(const_z, 4)
            g.affine_select(out=ident[:], in_=ident[:], compare_op=ALU.not_equal, fill=1.0, base=0,
                            pattern=[[-1, P]], channel_multiplier=1).then_inc(const_done, 1)
            g.affine_select(out=before[:], in_=before[:], compare_op=ALU.is_gt, fill=0.0, base=0,
                            pattern=[[1, P]], channel_multiplier=-1).then_inc(const_done, 1)
            g.affine_select(out=head_mask[:], in_=head_mask[:], compare_op=ALU.is_ge, fill=0.0, base=0,
                            pattern=[[-HD, HEADS], [0, HD]], channel_multiplier=1).then_inc(const_z, 1)
            g.affine_select(out=head_sel[:], in_=head_sel[:], compare_op=ALU.is_ge, fill=0.0, base=0,
                            pattern=[[-HD, HEADS]], channel_multiplier=1).then_inc(const_z, 1)
            pool.wait_ge(const_z, 6)
            g.affine_select(out=head_mask[:], in_=head_mask[:], compare_op=ALU.is_ge, fill=0.0, base=HD - 1,
                            pattern=[[HD, HEADS], [0, HD]], channel_multiplier=-1).then_inc(const_done, 1)
            g.affine_select(out=head_sel[:], in_=head_sel[:], compare_op=ALU.is_ge, fill=0.0, base=HD - 1,
                            pattern=[[HD, HEADS]], channel_multiplier=-1).then_inc(const_done, 1)
            g.iota(first_e[:], pattern=[[0, TILES], [-1, E]], base=E, channel_multiplier=0,
                   allow_small_or_imprecise_dtypes=True).then_inc(const_done, 1)
            g.iota(base_e[:], pattern=[[0, TILES], [CAP, E]], base=int(FAR), channel_multiplier=0,
                   allow_small_or_imprecise_dtypes=True).then_inc(const_done, 1)
            for u in range(2):
                g.iota(pay[:, u, :, D + E].bitcast(I32), pattern=[[1, TILES]], base=(u - 2) * S,
                       channel_multiplier=TILES).then_inc(payload_ids, 1)

            def send(b):
                for t in range(TILES):
                    for k in range(TOP):
                        if t == 0 and k == 0:
                            pool.wait_ge(empty_stored, E * ON_QUEUE)
                            pool.wait_ge(spots_ready, b.n + 1)
                            pool.sem_inc(pool_going, 1)
                        g.indirect_dma_start(
                            out=places, out_offset=bass.IndirectOffsetOnAxis(ap=spot[:, b.u, k, t:t + 1], axis=0),
                            in_=pay[:, b.u, t, :], in_offset=None, bounds_check=E * CAP - 1,
                            oob_is_err=False).then_inc(sent[b.u], ON_QUEUE)

            with pool.Fori(0, NB // 2) as i:
                for u in range(2):
                    send(Seq(i * 2 + u, u, i))

            def add(e):
                if e.u == 1:
                    pool.wait_ge(added[0], (e.half + 1) * (ET * ON_QUEUE))
                else:
                    pool.wait_ge(added[1], e.half * (ET * ON_QUEUE))
                for m in range(NCH):
                    pool.wait_ge(x1_stored, NB * ON_QUEUE)
                    pool.wait_ge(yo_ready, e.n * NCH + (m + 1))
                    pool.sem_inc(pool_going, 1)
                    for k in range(PAIR):
                        t = m * PAIR + k
                        g.indirect_dma_start(
                            out=out_rows,
                            out_offset=bass.IndirectOffsetOnAxis(ap=rows[:, e.u, t, D + E:PAY].bitcast(I32), axis=0),
                            in_=yo[:, e.u, t, :], in_offset=None, bounds_check=NB * S - 1, oob_is_err=False,
                            compute_op=ALU.add).then_inc(added[e.u], ON_QUEUE)

            run_experts(pool, add)
            for u in range(2):
                pool.wait_ge(added[u], E // 2 * ET * ON_QUEUE)

        @block.tensor
        def _(pe):
            mm, turn = nc.tensor.matmul, nc.tensor.transpose
            pe.wait_ge(const_done, 7)
            pe.wait_ge(w_in, 3 * ON_QUEUE)
            for c in range(4):
                turn(b_t0[:, c * P:(c + 1) * P], w_raw[:, c, :], ident[:])
            turn(b_t1[:, 0:E], wr_raw[:], ident[0:E, 0:E]).then_inc(w_turned, 1)

            def step(b, t):
                n_, a, bb, c_ = stages(b, t)

                def turn_x(c):
                    if c == 0:
                        pe.wait_ge(xn_ready, a.n + 1)
                        wait(pe, x1t_ready[1], a.n - 2)
                    else:
                        wait(pe, ot_ready[1], a.n - 1)
                    dst = b_t1 if c else b_t0
                    for k in range(TC):
                        ins = turn(dst[:, k * P:(k + 1) * P], xn[:, c * TC + k, 0:D], ident[:])
                    ins.then_inc(x_turned[c], 1)

                def make_o(c):
                    if c == 0:
                        pe.wait_ge(kvn_ready, bb.n + 1)
                    pe.wait_ge(phiq_ready, bb.n * CH + (c + 1))
                    wait(pe, o_ready, bb.n * CH + c)
                    for k in range(TC):
                        ins = mm(o_bank[k // 2][:, (k % 2) * 256:(k % 2) * 256 + ON],
                                 phiqt[:, c, k * P:(k + 1) * P], kvn[:], start=True, stop=True)
                    ins.then_inc(o_made, 1)

                def turn_x1(c):
                    if c == 0:
                        pe.wait_ge(pay_x, c_.n + 1)
                        wait(pe, xt_ready[0], c_.n + 3, NB)
                    else:
                        pe.wait_ge(x1t_ready[0], c_.n + 1)
                    for k in range(TC):
                        ins = turn(b_t0[:, k * P:(k + 1) * P], pay[:, c_.u, c * TC + k, 0:D], ident[:])
                    ins.then_inc(x1_turned[c], 1)

                def make_kq(c):
                    pe.wait_ge(xt_ready[c], a.n + 1)
                    wait(pe, phik_ready, a.n * CH + c)
                    for k in range(TC):
                        ins = mm(b_k[:, k * P:(k + 1) * P], xt[:, c, k * P:(k + 1) * P], w_t[:, 1, :],
                                 start=True, stop=True)
                    ins.then_inc(k_made, 1)
                    wait(pe, phiq_ready, a.n * CH + c)
                    mm(b_q[:], w_t[:, 0, :], xt[:, c, :], start=True, stop=True).then_inc(q_made, 1)

                def turn_o(c):
                    pe.wait_ge(o_ready, bb.n * CH + (c + 1))
                    if c == 0:
                        wait(pe, xt_ready[1], bb.n + 2, NB)
                    else:
                        pe.wait_ge(ot_ready[0], bb.n + 1)
                    for k in range(TC):
                        ins = turn(b_t1[:, k * P:(k + 1) * P], on[:, c, k * P:(k + 1) * P], ident[:])
                    ins.then_inc(o_turned[c], 1)

                def route(c):
                    pe.wait_ge(x1t_ready[c], c_.n + 1)
                    if c == 0:
                        wait(pe, spots_ready, c_.n)
                        pe.wait_ge(x1_ready, c_.n * CH + CH)
                    for k in range(TC):
                        j = c * TC + k
                        ins = mm(b_y[:, j * E:(j + 1) * E], x1t[:, c, k * P:(k + 1) * P], wr_t[:],
                                 start=True, stop=True)
                    if c == 1:
                        ins.then_inc(logits_made, 1)

                def make_g(c):
                    pe.wait_ge(phik_ready, a.n * CH + (c + 1))
                    if c == 0:
                        wait(pe, kvn_ready, a.n)
                    for k in range(TC):
                        ins = mm(b_g[:, 0:D + 1], phik[:, c, k * P:(k + 1) * P], xn[:, c * TC + k, :],
                                 start=(c == 0 and k == 0), stop=(c == 1 and k == TC - 1))
                    ins.then_inc(g_made if c else g_half, 1)

                def make_y(c):
                    pe.wait_ge(ot_ready[c], bb.n + 1)
                    if c == 0:
                        wait(pe, logits_kept, bb.n)
                    else:
                        pe.wait_ge(x1_ready, bb.n * CH + 1)
                    for k in range(TC):
                        ins = mm(b_y[:, k * P:(k + 1) * P], ot[:, c, k * P:(k + 1) * P], w_t[:, 3, :],
                                 start=True, stop=True)
                    ins.then_inc(y_made, 1)

                def positions():
                    pe.wait_ge(mask_ready, c_.n + 1)
                    wait(pe, x1_ready, (c_.n + 2) * CH, NB * CH)
                    pos = b_y[:, POS0:2 * POS0].rearrange("p (t e) -> p t e", e=E)
                    mm(pos, ones_bf[:], seen_bf[:].rearrange("p (a e) -> p a e", a=1).to_broadcast([P, TILES, E]),
                       start=True, stop=False)
                    for j in range(TILES):
                        m = mask_bf[:, j:j + 1, :]
                        if j < TILES - 1:
                            mm(pos[:, j + 1:, :], ident_bf[:], m.to_broadcast([P, TILES - 1 - j, E]),
                               start=False, stop=False)
                        ins = mm(pos, before[:], m.to_broadcast([P, TILES, E]), start=False, stop=(j == TILES - 1))
                    ins.then_inc(pos_made, 1)

                if a:
                    turn_x(0)
                if bb:
                    make_o(0)
                if a:
                    turn_x(1)
                if c_:
                    turn_x1(0)
                if a:
                    make_kq(0)
                if bb:
                    turn_o(0)
                if c_:
                    route(0)
                if bb:
                    make_o(1)
                if c_:
                    turn_x1(1)
                if a:
                    make_kq(1)
                    make_g(0)
                if c_:
                    route(1)
                if bb:
                    turn_o(1)
                    make_y(0)
                if a:
                    make_g(1)
                if bb:
                    make_y(1)
                if a:
                    pe.wait_ge(g_kept, a.n + 1)
                    turn(b_g[:, GT0:GT0 + P], g_sb[:, 0:D], ident[:]).then_inc(g_turned, 1)
                if c_:
                    positions()
                if a:
                    pe.wait_ge(gt_kept, a.n + 1)
                    mm(b_g[:, KV0:KV0 + P], gt_sb[:], w_t[:, 2, :], start=True, stop=True).then_inc(kv_made, 1)

            pe.wait_ge(w_kept, 1)
            run(pe, step)

            pe.wait_ge(spots_ready, NB)

            def expert(e):
                def turn_rows(m):
                    if m == 0:
                        pe.wait_ge(rows_in[e.u], (e.half + 1) * ON_QUEUE)
                    wait(pe, rt_ready, e.n * NCH + (m - 1))
                    for k in range(PAIR):
                        ins = turn(bank[(e.u * NCH + m) % 2][:, k * P:(k + 1) * P],
                                   rows[:, e.u, m * PAIR + k, 0:D], ident[:])
                    ins.then_inc(r_turned, 1)

                def hidden(m):
                    if m == 0:
                        pe.wait_ge(w1_in[e.u], (e.half + 1) * ON_QUEUE)
                    pe.wait_ge(rt_ready, e.n * NCH + (m + 1))
                    v = (e.u * NCH + m) % 2
                    for i in range(IB):
                        ins = mm(bank[2 + 2 * v + i // 2][:, (i % 2) * 256:(i % 2) * 256 + PAIR * P],
                                 w1[:, e.u, i * P:(i + 1) * P], rt_t[:, v, :], start=True, stop=True)
                    ins.then_inc(h_made, 1)

                def expert_out(m):
                    if m == 0:
                        pe.wait_ge(w2_in[e.u], (e.half + 1) * ON_QUEUE)
                    pe.wait_ge(h_act, e.n * NCH + (m + 1))
                    pe.wait_ge(h_dve, e.n * NCH + (m + 1))
                    wait(pe, yo_ready, e.n * NCH + (m - 1))
                    v = (e.u * NCH + m) % 2
                    for k in range(PAIR):
                        for i in range(IB):
                            ins = mm(bank[6 + v][:, k * P:(k + 1) * P], hid[:, v, i, k * P:(k + 1) * P],
                                     w2[:, e.u, i, :], start=(i == 0), stop=(i == IB - 1))
                    ins.then_inc(e_made, 1)
                return turn_rows, hidden, expert_out

            def pair(experts):
                chunks = [(expert(e), m) for e in experts for m in range(NCH)]
                for j, ((turn_rows, hidden, expert_out), m) in enumerate(chunks):
                    if j == 0:
                        turn_rows(m)
                    if j + 1 < len(chunks):
                        chunks[j + 1][0][0](chunks[j + 1][1])
                    hidden(m)
                    if j:
                        chunks[j - 1][0][2](chunks[j - 1][1])
                expert_out(m)

            run_pairs(pe, pair)

        @block.scalar
        def _(act):
            f = nc.scalar.activation

            def step(b, t):
                n_, a, bb, c_ = stages(b, t)

                def keep_xt(c):
                    act.wait_ge(x_turned[c], a.n + 1)
                    wait(act, q_made, (a.n - 1) * CH + (c + 1))
                    nc.scalar.copy(xt[:, c, :], (b_t1 if c else b_t0)[:]).then_inc(xt_ready[c], 1)

                def keep_x1t(c):
                    act.wait_ge(x1_turned[c], c_.n + 1)
                    wait(act, logits_made, c_.n)
                    nc.scalar.copy(x1t[:, c, :], b_t0[:]).then_inc(x1t_ready[c], 1)

                def keep_ot(c):
                    act.wait_ge(o_turned[c], bb.n + 1)
                    wait(act, y_made, (bb.n - 1) * CH + (c + 1))
                    nc.scalar.copy(ot[:, c, :], b_t1[:]).then_inc(ot_ready[c], 1)

                def exps_kq(c):
                    for made, relu, done, ready, src, dst in (
                            (k_made, k_relu, k_exp, phik_ready, b_k, kx), (q_made, q_relu, q_exp, phiq_ready, b_q, qx)):
                        act.wait_ge(made, a.n * CH + (c + 1))
                        wait(act, ready, (a.n - 1) * CH + (c + 1))
                        f(dst[:, c, :], src[:], ACT.Relu, scale=-1.0).then_inc(relu, 1)
                    for relu, done, dst in ((k_relu, k_exp, kx), (q_relu, q_exp, qx)):
                        act.wait_ge(relu, a.n * CH + (c + 1))
                        f(dst[:, c, :], dst[:, c, :], ACT.Exp, scale=-1.0).then_inc(done, 1)

                def rough_root(s, ln, var, log, root):
                    act.wait_ge(var, s.n + 1)
                    f(ln[:, 5, :], ln[:, 4, :], ACT.Ln).then_inc(log, 1)
                    act.wait_ge(log, s.n + 1)
                    f(ln[:, 6, :], ln[:, 5, :], ACT.Exp, scale=-0.5).then_inc(root, 1)

                if a:
                    keep_xt(0)
                    keep_xt(1)
                if c_:
                    keep_x1t(0)
                if a:
                    exps_kq(0)
                if bb:
                    keep_ot(0)
                if c_:
                    keep_x1t(1)
                if a:
                    exps_kq(1)
                if bb:
                    keep_ot(1)
                if c_:
                    act.wait_ge(shifted, c_.n + 1)
                    f(rt[:, 1], rt[:, 1], ACT.Exp).then_inc(exps, 1)
                if a:
                    act.wait_ge(g_made, a.n + 1)
                    wait(act, kvn_ready, a.n)
                    nc.scalar.copy(g_sb[:], b_g[:, 0:D + 1]).then_inc(g_kept, 1)
                    act.wait_ge(g_turned, a.n + 1)
                    nc.scalar.copy(gt_sb[:], b_g[:, GT0:GT0 + P]).then_inc(gt_kept, 1)
                if bb:
                    rough_root(bb, ln2, var2, ln2_log, root2)
                if n_:
                    rough_root(n_, ln1, var1, ln1_log, root1)
                if bb:
                    wait(act, sent[bb.u], bb.half * (TILES * TOP * ON_QUEUE))
                    act.wait_ge(ln2_ready, bb.n + 1)
                    for j in range(TILES):
                        ins = f(pay[:, bb.u, j, 0:D], x1[:, j, :], ACT.Identity, bias=ln2[:, 9, j:j + 1],
                                scale=ln2[:, 8, j:j + 1])
                    ins.then_inc(pay_x, 1)

            run(act, step)

            def expert(e):
                for m in range(NCH):
                    v = (e.u * NCH + m) % 2
                    act.wait_ge(r_turned, e.n * NCH + (m + 1))
                    wait(act, h_made, e.n * NCH + (m - 1))
                    nc.scalar.copy(rt_t[:, v, :], bank[v][:, 0:PAIR * P]).then_inc(rt_ready, 1)
                    act.wait_ge(h_made, e.n * NCH + (m + 1))
                    wait(act, e_made, e.n * NCH + (m - 1))
                    f(hid[:, v, 0:2, :].rearrange("p i n -> p (i n)"), bank[2 + 2 * v][:], ACT.Relu).then_inc(h_act, 1)

            run_experts(act, expert)

        @block.vector
        def _(dve):
            v = nc.vector
            v.memset(empty[:], 0.0).then_inc(empty_set, 1)
            dve.wait_ge(empty_set, 1)
            v.memset(empty[:, :, D + E].bitcast(I32), NB * S).then_inc(empty_set, 1)
            v.memset(xn[:, :, D:D + 1], 1.0)
            v.memset(seen[:], 0.0)
            v.memset(seen_bf[:], 0.0).then_inc(ones_set, 1)
            nch, bch, cch, och = (Chain(dve, n_chain, 7), Chain(dve, b_chain, 7), Chain(dve, c_chain, 20),
                                  Chain(dve, o_chain, 2 * CH))

            def spread(ch, st, ln, var):
                v.tensor_tensor(ln[:, 0, :], st[:, :, 1], st[:, :, 4], ALU.add)
                v.tensor_tensor(ln[:, 1, :], st[:, :, 1], st[:, :, 4], ALU.subtract)
                ch.link(v.tensor_tensor(ln[:, 3, :], st[:, :, 2], st[:, :, 5], ALU.add))
                v.tensor_scalar(ln[:, 2, :], ln[:, 0, :], 0.5, None, ALU.mult)
                ch.link(v.tensor_tensor(ln[:, 1, :], ln[:, 1, :], ln[:, 1, :], ALU.mult))
                ch.link(v.scalar_tensor_tensor(out=ln[:, 3, :], in0=ln[:, 1, :], scalar=D / 4.0, in1=ln[:, 3, :],
                                               op0=ALU.mult, op1=ALU.add))
                v.tensor_scalar(ln[:, 4, :], ln[:, 3, :], 1.0 / D, LN_EPS, ALU.mult, ALU.add).then_inc(var, 1)

            def newton(ch, ln):
                ch.link(v.tensor_tensor(ln[:, 7, :], ln[:, 6, :], ln[:, 6, :], ALU.mult))
                ch.link(v.scalar_tensor_tensor(out=ln[:, 7, :], in0=ln[:, 7, :], scalar=-0.5, in1=ln[:, 4, :],
                                               op0=ALU.mult, op1=ALU.mult))
                ch.link(v.scalar_tensor_tensor(out=ln[:, 8, :], in0=ln[:, 7, :], scalar=1.5, in1=ln[:, 6, :],
                                               op0=ALU.add, op1=ALU.mult))

            def step(b, t):
                n_, a, bb, c_ = stages(b, t)

                def normalise_o(c):
                    dve.wait_ge(o_made, bb.n * CH + (c + 1))
                    wait(dve, o_turned[c], bb.n)
                    for h in range(2):
                        src = o_bank[h][:].rearrange("p (k n) -> p k n", n=256)[:, :, D:ON]
                        ins = v.tensor_scalar(nrm[:, c, h * 2 * HEADS:(h + 1) * 2 * HEADS].rearrange("p (k n) -> p k n", k=2),
                                              src, NORM_MIN, None, ALU.max)
                    och.link(ins)
                    och.link(v.reciprocal(rnrm[:, c, :], nrm[:, c, :]))
                    for h in range(2):
                        src = o_bank[h][:].rearrange("p (k n) -> p k n", n=256)[:, :, 0:D]
                        r = rnrm[:, c, h * 2 * HEADS:(h + 1) * 2 * HEADS].rearrange("p (k h a) -> p k h a", k=2, a=1)
                        ins = v.tensor_tensor(
                            on[:, c, h * 256:(h + 1) * 256].rearrange("p (k h j) -> p k h j", k=2, j=HD),
                            src.rearrange("p k (h j) -> p k h j", j=HD), r.to_broadcast([P, 2, HEADS, HD]), ALU.mult)
                    ins.then_inc(o_ready, 1)

                def feature_map(c):
                    dve.wait_ge(k_exp, a.n * CH + (c + 1))
                    wait(dve, g_made if c else g_half, a.n)
                    v.scalar_tensor_tensor(out=phik[:, c, :], in0=b_k[:], scalar=0.0, in1=kx[:, c, :],
                                           op0=ALU.max, op1=ALU.add).then_inc(phik_ready, 1)
                    dve.wait_ge(q_exp, a.n * CH + (c + 1))
                    wait(dve, o_made, (a.n - 1) * CH + (c + 1))
                    v.scalar_tensor_tensor(out=phiqt[:, c, :], in0=b_q[:], scalar=0.0, in1=qx[:, c, :],
                                           op0=ALU.max, op1=ALU.add).then_inc(phiq_ready, 1)

                def residual(c):
                    dve.wait_ge(y_made, bb.n * CH + (c + 1))
                    if c == 0:
                        wait(dve, x1_stored, bb.n * ON_QUEUE)
                        wait(dve, pay_x, bb.n)
                    v.tensor_tensor(x1[:, c * TC:(c + 1) * TC, :], b_y[:].rearrange("p (t d) -> p t d", d=D),
                                    xs[:, bb.n, c * TC:(c + 1) * TC, :], ALU.add).then_inc(x1_ready, 1)
                    dve.wait_ge(x1_ready, bb.n * CH + (c + 1))
                    for k in range(TC):
                        ins = v.bn_stats(st2[:, c * TC + k, :], x1[:, c * TC + k, :])
                    if c == 1:
                        bch.link(ins)
                        spread(bch, st2, ln2, var2)

                def wide(m):
                    return m.rearrange("p (t a) -> p t a", a=1).to_broadcast([P, TILES, E])

                def choose_first():
                    cch.begin(c_)
                    dve.wait_ge(logits_made, c_.n + 1)
                    v.tensor_tensor(rt[:, 0], b_y[:, 0:TILES * E].rearrange("p (t e) -> p t e", e=E),
                                    bias_e[:].rearrange("p (a e) -> p a e", a=1).to_broadcast([P, TILES, E]),
                                    ALU.add).then_inc(logits_kept, 1)
                    dve.wait_ge(logits_kept, c_.n + 1)
                    cch.link(v.tensor_reduce(rm[:, 0, :], rt[:, 0], AX.X, ALU.max))
                    v.tensor_tensor(rt[:, 1], rt[:, 0], wide(rm[:, 0, :]), ALU.subtract).then_inc(shifted, 1)
                    cch.link(v.tensor_tensor(rt[:, 3], rt[:, 0], wide(rm[:, 0, :]), ALU.is_equal))
                    cch.link(v.tensor_tensor(rt[:, 3], rt[:, 3], first_e[:], ALU.mult))
                    cch.link(v.tensor_reduce(rm[:, 1, :], rt[:, 3], AX.X, ALU.max))
                    cch.link(v.tensor_tensor(rt[:, 5], rt[:, 3], wide(rm[:, 1, :]), ALU.is_equal))
                    cch.link(v.scalar_tensor_tensor(out=rt[:, 7], in0=rt[:, 5], scalar=NO_LOGIT, in1=rt[:, 0],
                                                    op0=ALU.mult, op1=ALU.add))
                    cch.link(v.tensor_reduce(rm[:, 2, :], rt[:, 7], AX.X, ALU.max))
                    cch.link(v.tensor_tensor(rt[:, 4], rt[:, 7], wide(rm[:, 2, :]), ALU.is_equal))
                    cch.link(v.tensor_tensor(rt[:, 4], rt[:, 4], first_e[:], ALU.mult))
                    cch.link(v.tensor_reduce(rm[:, 3, :], rt[:, 4], AX.X, ALU.max))
                    cch.link(v.tensor_tensor(rt[:, 6], rt[:, 4], wide(rm[:, 3, :]), ALU.is_equal))
                    v.tensor_tensor(rt[:, 8], rt[:, 5], rt[:, 6], ALU.add)

                def weigh():
                    dve.wait_ge(exps, c_.n + 1)
                    cch.link(v.tensor_reduce(rm[:, 4, :], rt[:, 1], AX.X, ALU.add))
                    cch.link(v.reciprocal(rm[:, 5, :], rm[:, 4, :]))
                    cch.link(v.tensor_tensor(rt[:, 2], rt[:, 1], wide(rm[:, 5, :]), ALU.mult))
                    wait(dve, pos_made, c_.n)
                    cch.link(v.scalar_tensor_tensor(out=mask_bf[:], in0=rt[:, 2], scalar=0.0, in1=rt[:, 8],
                                                    op0=ALU.is_gt, op1=ALU.mult))
                    v.tensor_copy(seen_bf[:], seen[:]).then_inc(mask_ready, 1)
                    v.tensor_copy(pay[:, c_.u, :, D:D + E], rt[:, 2])
                    v.tensor_scalar(pay[:, c_.u, :, D + E].bitcast(I32), pay[:, c_.u, :, D + E].bitcast(I32),
                                    2 * S, None, ALU.add)
                    v.tensor_reduce(rm[:, 6, :], mask_bf[:].rearrange("p t e -> p e t"), AX.X, ALU.add)
                    cch.link(v.scalar_tensor_tensor(out=rt[:, 9], in0=mask_bf[:], scalar=-FAR, in1=base_e[:],
                                                    op0=ALU.mult, op1=ALU.add))

                def find_places():
                    dve.wait_ge(pos_made, c_.n + 1)
                    pos = b_y[:, POS0:2 * POS0].rearrange("p (t e) -> p t e", e=E)
                    v.tensor_tensor(seen[:], seen[:], rm[:, 6, :], ALU.add)
                    v.tensor_scalar(rt[:, 10], pos, float(CAP), FAR, ALU.is_ge, ALU.mult)
                    cch.link(v.tensor_tensor(rt[:, 11], pos, rt[:, 9], ALU.add))
                    cch.link(v.tensor_tensor(rt[:, 12], rt[:, 11], rt[:, 10], ALU.add))
                    cch.link(v.tensor_tensor(
                        rt[:, 13:15].rearrange("p k t e -> p k (t e)"), rt[:, 5:7].rearrange("p k t e -> p k (t e)"),
                        rt[:, 12:13].rearrange("p k t e -> p k (t e)").to_broadcast([P, TOP, TILES * E]), ALU.mult))
                    cch.link(v.tensor_reduce(choice[:], rt[:, 13:15], AX.X, ALU.add))
                    v.tensor_copy(spot[:, c_.u], choice[:]).then_inc(spots_ready, 1)
                    cch.end()

                if bb:
                    och.begin(bb)
                    normalise_o(0)
                if a:
                    feature_map(0)
                if bb:
                    normalise_o(1)
                if c_:
                    choose_first()
                if a:
                    feature_map(1)
                if bb:
                    bch.begin(bb)
                    residual(0)
                if c_:
                    weigh()
                if bb:
                    residual(1)
                if n_:
                    nch.begin(n_)
                    dve.wait_ge(x_in[n_.u], (n_.half + 1) * ON_QUEUE)
                    for k in range(TILES):
                        ins = v.bn_stats(st1[:, k, :], xs[:, n_.n, k, :])
                    nch.link(ins)
                    spread(nch, st1, ln1, var1)
                if a:
                    dve.wait_ge(kv_made, a.n + 1)
                    wait(dve, o_made, a.n * CH)
                    v.tensor_tensor(kvn[:, 0:D], b_g[:, KV0:KV0 + P], head_mask[:].rearrange("p h j -> p (h j)"),
                                    ALU.mult)
                    v.tensor_scalar(kvn[:, D:ON], head_sel[:], g_sb[:, D:D + 1], None, ALU.mult).then_inc(kvn_ready, 1)
                if c_:
                    find_places()
                if bb:
                    dve.wait_ge(root2, bb.n + 1)
                    newton(bch, ln2)
                    bch.end()
                    v.scalar_tensor_tensor(out=ln2[:, 9, :], in0=ln2[:, 2, :], scalar=-1.0, in1=ln2[:, 8, :],
                                           op0=ALU.mult, op1=ALU.mult).then_inc(ln2_ready, 1)
                if n_:
                    dve.wait_ge(root1, n_.n + 1)
                    newton(nch, ln1)
                    nch.end()
                    wait(dve, g_made, n_.n)
                    for k in range(TILES):
                        ins = v.tensor_scalar(xn[:, k, 0:D], xs[:, n_.n, k, :], ln1[:, 2, k:k + 1],
                                              ln1[:, 8, k:k + 1], ALU.subtract, ALU.mult)
                    ins.then_inc(xn_ready, 1)

            dve.wait_ge(w_turned, 1)
            v.tensor_copy(w_t[:].rearrange("p c d -> p (c d)"), b_t0[:])
            v.tensor_copy(wr_t[:], b_t1[:, 0:E])
            dve.wait_ge(const_done, 7)
            dve.wait_ge(wr_in, ON_QUEUE)
            dve.wait_ge(payload_ids, 2)
            dve.wait_ge(ones_set, 1)
            v.tensor_copy(ident_bf[:], ident[:]).then_inc(w_kept, 1)
            run(dve, step)

            def expert(e):
                for m in range(NCH):
                    w = (e.u * NCH + m) % 2
                    dve.wait_ge(h_made, e.n * NCH + (m + 1))
                    wait(dve, e_made, e.n * NCH + (m - 1))
                    v.tensor_scalar(hid[:, w, 2:4, :].rearrange("p i n -> p (i n)"), bank[3 + 2 * w][:], 0.0, None,
                                    ALU.max).then_inc(h_dve, 1)
                    dve.wait_ge(e_made, e.n * NCH + (m + 1))
                    if m == 0:
                        wait(dve, added[e.u], e.half * (ET * ON_QUEUE))
                    for k in range(PAIR):
                        j = m * PAIR + k
                        ins = v.tensor_scalar(yo[:, e.u, j, :], bank[6 + w][:, k * P:(k + 1) * P],
                                              rows[:, e.u, j, bass.ds(e.n + D, 1)], None, ALU.mult)
                    ins.then_inc(yo_ready, 1)

            run_experts(dve, expert)


_INS = ["L0_attn_x", "L0_attn_w_qkv", "L0_attn_w_out", "L0_ffn_W_router", "L0_ffn_b_router",
        "L0_ffn_experts_inter", "L0_ffn_experts_out"]
_OUTS = [((8, 1024, 128), "float32")]


def kernel(**inputs):
    import numpy as _np
    import concourse.bacc as _bacc
    from concourse import mybir as _mybir
    from concourse.bass_utils import run_bass_kernel_spmd as _run

    nc = _bacc.Bacc("TRN2", target_bir_lowering=False, num_devices=1)
    arrays, args = {}, []
    for name in _INS:
        a = _np.ascontiguousarray(inputs[name])
        arrays[f"in_{name}_dram"] = a
        args.append(nc.dram_tensor(f"in_{name}_dram", a.shape, _mybir.dt.from_np(a.dtype), kind="ExternalInput").ap())
    for i, (shape, dtype) in enumerate(_OUTS):
        dt = _mybir.dt.from_np(_np.dtype(dtype))
        args.append(nc.dram_tensor(f"out_{i}_dram", shape, dt, kind="ExternalOutput").ap())
    moe_layer(nc, *args)
    r = _run(nc, [arrays], core_ids=[0])
    got = tuple(r.results[0][f"out_{i}_dram"] for i in range(len(_OUTS)))
    return got[0]
```

```python
from contextlib import ExitStack

import concourse.bass as bass
from concourse import mybir

F32 = mybir.dt.float32
F32R = mybir.dt.float32r
BF16 = mybir.dt.bfloat16
I32 = mybir.dt.int32
U32 = mybir.dt.uint32
ALU = mybir.AluOpType
ACT = mybir.ActivationFunctionType
AX = mybir.AxisListType

P = 128
HEADS = 16
TOP = 2
LN_EPS = 1e-5
NORM_MIN = 1e-6
ON_QUEUE = 16
FAR = 16384.0


class Seq:

    def __init__(self, n, parity, half):
        self.n, self.u, self.half = n, parity, half

    @staticmethod
    def fixed(n):
        return Seq(n, n % 2, n // 2)

    def shift(self, k):
        if isinstance(self.n, int):
            return Seq.fixed(self.n + k)
        v = self.u + k
        return Seq(self.n + k, v % 2, self.half + v // 2)


def wait(eng, sem, value, most=None):
    if isinstance(value, int):
        if most is not None:
            value = min(value, most)
        if value <= 0:
            return
    eng.wait_ge(sem, value)


class Chain:

    def __init__(self, eng, sem, per, first=0):
        self.eng, self.sem, self.per, self.first = eng, sem, per, first

    def begin(self, b):
        self.base, self.j = (b.n - self.first) * self.per, 0

    def link(self, ins):
        self.j += 1
        assert self.j <= self.per
        ins.then_inc(self.sem, 1)
        self.eng.wait_ge(self.sem, self.base + self.j)

    def end(self):
        assert self.j == self.per, (self.j, self.per)


def moe_layer(nc, x, w_qkv, w_out, w_router, b_router, w_inter, w_exp_out, out):
    NB, S, D = x.shape
    E, _, I = w_inter.shape
    TILES = S // P
    CH = 2
    TC = TILES // CH
    HD = D // HEADS
    CAP = -(-NB * S * 5 // (E * 4))
    ET = CAP // P
    PAIR = 2
    NCH = ET // PAIR
    IB = I // P
    PAY = D + E + 1
    ON = D + HEADS
    AHEAD = 2
    assert D == P and CAP % P == 0 and ET % PAIR == 0 and TC * P == 512

    x_v = x.rearrange("b (p t) d -> b p (t d)", p=P)
    out_v = out.rearrange("b (p t) d -> b p (t d)", p=P)
    out_rows = out.rearrange("b s d -> (b s) d")
    places = nc.dram_tensor("places", [E * CAP, PAY], F32).ap()
    places_v = places.rearrange("(e p t) c -> e p (t c)", e=E, p=P)
    w2_v = w_exp_out.rearrange("e (c p) h -> e p c h", p=P)

    with ExitStack() as ctx:
        def sb(name, shape, dt=F32):
            return ctx.enter_context(nc.sbuf_tensor(name, shape, dt))

        def sem(name):
            return ctx.enter_context(nc.semaphore(name))

        bank = [ctx.enter_context(nc.psum_tensor(f"bank{i}", [P, 512], F32)) for i in range(8)]

        ident = sb("ident", [P, P])
        ident_bf = sb("ident_bf", [P, P], BF16)
        before = sb("before", [P, P], BF16)
        ones_bf = sb("ones_bf", [P, P], BF16)
        head_mask = sb("head_mask", [P, HEADS, HD])
        head_sel = sb("head_sel", [P, HEADS])
        number_e = sb("number_e", [P, TILES, E])
        base_e = sb("base_e", [P, TILES, E])
        bias_e = sb("bias_e", [P, E])
        w_raw = sb("w_raw", [P, 4, P])
        wr_raw = sb("wr_raw", [E, P])
        w_t = sb("w_t", [P, 4, P])
        wr_t = sb("wr_t", [P, E])
        ones_f = sb("ones_f", [P, P])
        minus_one = sb("minus_one", [P, 1])
        wr_sum = sb("wr_sum", [P, E])
        empty = sb("empty", [P, ET, PAY])
        xs = sb("xs", [P, NB, TILES, D])
        stats = sb("stats", [P, 2 * TILES, 6])
        ln = sb("ln", [P, 2, 10, 2 * TILES])
        xn = sb("xn", [P, 2, TILES, D + 1])
        xt = sb("xt", [P, CH, 512])
        kx = sb("kx", [P, CH, 512])
        qx = sb("qx", [P, CH, 512])
        phik = sb("phik", [P, CH, 512])
        phiqt = sb("phiqt", [P, 2, CH, 512])
        g_sb = sb("g_sb", [P, D + 1])
        gt_sb = sb("gt_sb", [P, D])
        kvn = sb("kvn", [P, ON])
        nrm = sb("nrm", [P, CH, TC * HEADS])
        rnrm = sb("rnrm", [P, CH, TC * HEADS])
        on = sb("on", [P, CH, 512])
        ot = sb("ot", [P, CH, 512])
        x1 = sb("x1", [P, 2, TILES, D])
        pay = sb("pay", [P, 2, TILES, PAY])
        x1t = sb("x1t", [P, CH, 512])
        logit = sb("logit", [P, TILES, E])
        top_val = sb("top_val", [P, TILES, 8])
        top_idx = sb("top_idx", [P, TILES, 8], U32)
        expo = sb("expo", [P, TILES, E])
        total = sb("total", [P, 2, TILES])
        weight = sb("weight", [P, TILES, E])
        chosen = sb("chosen", [P, TOP, TILES, E])
        offset = sb("offset", [P, TILES, E])
        either = sb("either", [P, TILES, E])
        taken = sb("taken", [P, E])
        base_m = sb("base_m", [P, TILES, E])
        over = sb("over", [P, TILES, E])
        place = sb("place", [P, TILES, E])
        place_k = sb("place_k", [P, TOP, TILES, E])
        mask_bf = sb("mask_bf", [P, TILES, E], BF16)
        seen = sb("seen", [P, E], F32)
        seen_bf = sb("seen_bf", [P, E], BF16)
        choice = sb("choice", [P, TOP, TILES])
        spot = sb("spot", [P, 2, TOP, TILES], I32)
        rows = sb("rows", [P, 2, ET, PAY])
        w1 = sb("w1", [P, 2, I])
        w2 = sb("w2", [P, 2, IB, D])
        w1_hl = [sb(f"w1_{h}", [P, 2, I], F32R) for h in ("hi", "lo")]
        w2_hl = [sb(f"w2_{h}", [P, 2, IB, D], F32R) for h in ("hi", "lo")]
        rt_hl = [sb(f"rt_{h}", [P, 2, PAIR * P], F32R) for h in ("hi", "lo")]
        hid_hl = [sb(f"hid_{h}", [P, 2, IB, PAIR * P], F32R) for h in ("hi", "lo")]
        yt = sb("yt", [P, 2, PAIR * P])
        yo = sb("yo", [P, 2, ET, D])

        w_in, wr_in = sem("w_in"), sem("wr_in")
        x_in = [sem(f"x_in{u}") for u in range(2)]
        const_z, const_done, payload_ids = sem("const_z"), sem("const_done"), sem("payload_ids")
        empty_set, empty_stored = sem("empty_set"), sem("empty_stored")
        ones_set = sem("ones_set")
        wr_summed, wr_sum_kept = sem("wr_summed"), sem("wr_sum_kept")
        w_turned, w_kept = sem("w_turned"), sem("w_kept")
        spread_chain, newton_chain, var_ready, log_ready, root_ready, ln_ready, xn_ready = (
            sem(s) for s in ("spread_chain", "newton_chain", "var_ready", "log_ready", "root_ready", "ln_ready",
                             "xn_ready"))
        stats1_ready, stats2_ready = sem("stats1_ready"), sem("stats2_ready")
        x_turned = [sem(f"x_turned{c}") for c in range(CH)]
        xt_ready = [sem(f"xt_ready{c}") for c in range(CH)]
        k_made, q_made = sem("k_made"), sem("q_made")
        k_exp, q_exp = sem("k_exp"), sem("q_exp")
        phik_ready, phiq_ready = sem("phik_ready"), sem("phiq_ready")
        g_half, g_made, g_kept, g_turned, gt_kept, kv_made, kvn_ready = (
            sem(s) for s in ("g_half", "g_made", "g_kept", "g_turned", "gt_kept", "kv_made", "kvn_ready"))
        o_made, o_chain, o_ready = sem("o_made"), sem("o_chain"), sem("o_ready")
        o_turned = [sem(f"o_turned{c}") for c in range(CH)]
        ot_ready = [sem(f"ot_ready{c}") for c in range(CH)]
        y_made, x1_ready = sem("y_made"), sem("x1_ready")
        x1_stored = [sem(f"x1_stored{u}") for u in range(2)]
        x1_turned = [sem(f"x1_turned{c}") for c in range(CH)]
        x1t_ready = [sem(f"x1t_ready{c}") for c in range(CH)]
        logits_made, logits_kept, shifted, exps, mask_ready, pay_free, pay_x, places_read = (
            sem(s) for s in ("logits_made", "logits_kept", "shifted", "exps", "mask_ready", "pay_free", "pay_x",
                             "places_read"))
        offset_chain, choose_chain, weigh_chain, place_chain = (
            sem(s) for s in ("offset_chain", "choose_chain", "weigh_chain", "place_chain"))
        pool_going = sem("pool_going")
        pos_made, spots_ready = sem("pos_made"), sem("spots_ready")
        sent = [sem(f"sent{u}") for u in range(2)]
        rows_in = [sem(f"rows_in{u}") for u in range(2)]
        w1_in = [sem(f"w1_in{u}") for u in range(2)]
        w2_in = [sem(f"w2_in{u}") for u in range(2)]
        w_hi_ready, w_lo_ready, r_turned, rt_hi_ready, rt_lo_ready = (
            sem(s) for s in ("w_hi_ready", "w_lo_ready", "r_turned", "rt_hi_ready", "rt_lo_ready"))
        h_made, h_hi_ready, h_lo_ready, e_made, yt_ready, y_turned, yo_ready = (
            sem(s) for s in ("h_made", "h_hi_ready", "h_lo_ready", "e_made", "yt_ready", "y_turned", "yo_ready"))
        added = [sem(f"added{u}") for u in range(2)]

        b_t0, b_t1, b_k, b_q, b_g, b_o0, b_o1, b_y = bank
        o_bank = [b_o0, b_o1]
        b_t = [b_t0, b_t1]
        GT0, KV0 = 160, 320
        POS0 = TILES * E

        def run(eng, step, first, last, loop):
            def doer(b, t, last_t):
                def do(work, k, *part, first=0):
                    if t - k >= first and last_t - k < NB:
                        work(b.shift(-k), *part)
                return do

            for t in range(first, loop[0]):
                step(doer(Seq.fixed(t), t, t))
            with eng.Fori(0, (loop[1] - loop[0]) // 2) as i:
                for t in range(loop[0], loop[0] + 2):
                    step(doer(Seq(i * 2 + t, t % 2, i + t // 2), t, loop[1] - 2 + (t - loop[0])))
            for t in range(loop[1], last + 1):
                step(doer(Seq.fixed(t), t, t))

        def run_experts(eng, expert):
            def fixed(n):
                return Seq.fixed(n) if 0 <= n < E else None

            for n in (0, 1):
                expert(fixed(n - 1), fixed(n), fixed(n + 1))
            with eng.Fori(1, E // 2 - 1) as i:
                for u in range(2):
                    e = Seq(i * 2 + u, u, i)
                    expert(e.shift(-1), e, e.shift(1))
            for n in (E - 2, E - 1):
                expert(fixed(n - 1), fixed(n), fixed(n + 1))

        def walk(before, e, after, split, rows, hidden, late, last):
            chunks = {m: (e, m) for m in range(NCH)}
            for k in (1, 2):
                if before:
                    chunks[-k] = (before, NCH - k)
            if after:
                chunks[NCH] = (after, 0)
            if not before:
                split(e)
                rows(e, 0)
            for m in range(NCH):
                if m + 1 in chunks:
                    rows(*chunks[m + 1])
                hidden(e, m)
                if m - 2 in chunks:
                    last(*chunks[m - 2])
                if m - 1 in chunks:
                    late(*chunks[m - 1])
                if m == 1 and after:
                    split(after)
            if not after:
                last(*chunks[NCH - 2])
                late(e, NCH - 1)
                last(e, NCH - 1)

        def chunk(e, m):
            return e.n * NCH + m, (e.u * NCH + m) % 2

        block = ctx.enter_context(nc.Block())

        @block.sync
        def _(sp):
            def load_x(b):
                wait(sp, x_in[b.u], b.half * ON_QUEUE)
                sp.dma_start(xs[:, b.n].rearrange("p t d -> p (t d)"), x_v[b.n]).then_inc(x_in[b.u], ON_QUEUE)

            load_x(Seq.fixed(0))
            sp.dma_start(w_raw[:, 0:3, :], w_qkv.rearrange("(c p) d -> p c d", p=P)).then_inc(w_in, ON_QUEUE)
            sp.dma_start(w_raw[:, 3, :], w_out).then_inc(w_in, ON_QUEUE)
            sp.dma_start(wr_raw[:], w_router).then_inc(w_in, ON_QUEUE)
            sp.dma_start(bias_e[:], b_router.rearrange("(a e) -> a e", a=1).to_broadcast([P, E])).then_inc(wr_in, ON_QUEUE)
            load_x(Seq.fixed(1))
            sp.wait_ge(empty_set, 2)
            for e in range(E):
                sp.dma_start(places_v[e], empty[:].rearrange("p t c -> p (t c)")).then_inc(empty_stored, ON_QUEUE)
            with sp.Fori(1, NB // 2) as i:
                for u in range(2):
                    load_x(Seq(i * 2 + u, u, i))

            def load_weights(e):
                wait(sp, w_lo_ready, (e.half - 1) * 2 + (e.u + 1))
                sp.dma_start(w1[:, e.u], w_inter[e.n]).then_inc(w1_in[e.u], ON_QUEUE)
                sp.dma_start(w2[:, e.u], w2_v[e.n]).then_inc(w2_in[e.u], ON_QUEUE)

            def load_rows(e):
                wait(sp, added[e.u], e.half * ET * ON_QUEUE)
                sp.dma_start(rows[:, e.u].rearrange("p t c -> p (t c)"), places_v[e.n]).then_inc(rows_in[e.u], ON_QUEUE)

            for u in range(2):
                load_weights(Seq.fixed(u))
            with sp.Fori(0, NB // 2) as i:
                for u in range(2):
                    sp.wait_ge(x1_ready, (i * 2 + u) * CH + CH)
                    sp.dma_start(out_v[i * 2 + u], x1[:, u].rearrange("p t d -> p (t d)")).then_inc(x1_stored[u], ON_QUEUE)
            for u in range(2):
                sp.wait_ge(sent[u], NB // 2 * TILES * TOP * ON_QUEUE)
            for u in range(2):
                load_rows(Seq.fixed(u))
            with sp.Fori(1, E // 2) as i:
                for u in range(2):
                    load_weights(Seq(i * 2 + u, u, i))
                    load_rows(Seq(i * 2 + u, u, i))

        @block.gpsimd
        def _(pool):
            g = nc.gpsimd
            g.memset(ident[:], 0.0).then_inc(const_z, 1)
            g.memset(before[:], 1.0).then_inc(const_z, 1)
            g.memset(head_mask[:], 1.0).then_inc(const_z, 1)
            g.memset(head_sel[:], 1.0).then_inc(const_z, 1)
            g.memset(ones_bf[:], 1.0).then_inc(const_done, 1)
            g.memset(ones_f[:], 1.0).then_inc(const_done, 1)
            pool.wait_ge(const_z, 4)
            g.affine_select(out=ident[:], in_=ident[:], compare_op=ALU.not_equal, fill=1.0, base=0,
                            pattern=[[-1, P]], channel_multiplier=1).then_inc(const_done, 1)
            g.affine_select(out=before[:], in_=before[:], compare_op=ALU.is_gt, fill=0.0, base=0,
                            pattern=[[1, P]], channel_multiplier=-1).then_inc(const_done, 1)
            g.affine_select(out=head_mask[:], in_=head_mask[:], compare_op=ALU.is_ge, fill=0.0, base=0,
                            pattern=[[-HD, HEADS], [0, HD]], channel_multiplier=1).then_inc(const_z, 1)
            g.affine_select(out=head_sel[:], in_=head_sel[:], compare_op=ALU.is_ge, fill=0.0, base=0,
                            pattern=[[-HD, HEADS]], channel_multiplier=1).then_inc(const_z, 1)
            pool.wait_ge(const_z, 6)
            g.affine_select(out=head_mask[:], in_=head_mask[:], compare_op=ALU.is_ge, fill=0.0, base=HD - 1,
                            pattern=[[HD, HEADS], [0, HD]], channel_multiplier=-1).then_inc(const_done, 1)
            g.affine_select(out=head_sel[:], in_=head_sel[:], compare_op=ALU.is_ge, fill=0.0, base=HD - 1,
                            pattern=[[HD, HEADS]], channel_multiplier=-1).then_inc(const_done, 1)
            g.iota(number_e[:], pattern=[[0, TILES], [1, E]], base=0, channel_multiplier=0,
                   allow_small_or_imprecise_dtypes=True).then_inc(const_done, 1)
            g.iota(base_e[:], pattern=[[0, TILES], [CAP, E]], base=int(FAR), channel_multiplier=0,
                   allow_small_or_imprecise_dtypes=True).then_inc(const_done, 1)
            for u in range(2):
                g.iota(pay[:, u, :, D + E].bitcast(I32), pattern=[[1, TILES]], base=(u - 2) * S,
                       channel_multiplier=TILES).then_inc(payload_ids, 1)

            def send(b):
                for t in range(TILES):
                    for k in range(TOP):
                        if t == 0 and k == 0:
                            pool.wait_ge(empty_stored, E * ON_QUEUE)
                            pool.wait_ge(pay_x, b.n + 1)
                            pool.wait_ge(spots_ready, b.n + 1)
                            pool.sem_inc(pool_going, 1)
                        g.indirect_dma_start(
                            out=places, out_offset=bass.IndirectOffsetOnAxis(ap=spot[:, b.u, k, t:t + 1], axis=0),
                            in_=pay[:, b.u, t, :], in_offset=None, bounds_check=E * CAP - 1,
                            oob_is_err=False).then_inc(sent[b.u], ON_QUEUE)

            with pool.Fori(0, NB // 2) as i:
                for u in range(2):
                    send(Seq(i * 2 + u, u, i))

            def add(before, e, after):
                if before:
                    pool.wait_ge(added[before.u], (before.half + 1) * (ET * ON_QUEUE))
                for m in range(NCH):
                    for stored in x1_stored:
                        pool.wait_ge(stored, NB // 2 * ON_QUEUE)
                    pool.wait_ge(yo_ready, e.n * NCH + (m + 1))
                    pool.sem_inc(pool_going, 1)
                    for k in range(PAIR):
                        t = m * PAIR + k
                        g.indirect_dma_start(
                            out=out_rows,
                            out_offset=bass.IndirectOffsetOnAxis(ap=rows[:, e.u, t, D + E:PAY].bitcast(I32), axis=0),
                            in_=yo[:, e.u, t, :], in_offset=None, bounds_check=NB * S - 1, oob_is_err=False,
                            compute_op=ALU.add).then_inc(added[e.u], ON_QUEUE)

            run_experts(pool, add)
            for u in range(2):
                pool.wait_ge(added[u], E // 2 * ET * ON_QUEUE)

        @block.tensor
        def _(pe):
            mm, turn = nc.tensor.matmul, nc.tensor.transpose
            pe.wait_ge(const_done, 8)
            pe.wait_ge(w_in, 3 * ON_QUEUE)
            for c in range(4):
                turn(b_t0[:, c * P:(c + 1) * P], w_raw[:, c, :], ident[:])
            turn(b_t1[:, 0:E], wr_raw[:], ident[0:E, 0:E]).then_inc(w_turned, 1)

            def plus_one(b_out):
                mm(b_out[:].rearrange("p (k n) -> p k n", n=P), ones_bf[0:1, :],
                   ones_bf[0:1, :].rearrange("p (a n) -> p a n", a=1).to_broadcast([1, TC, P]), start=True, stop=False)

            def turn_x(s, c):
                pe.wait_ge(xn_ready, s.n * CH + (c + 1))
                wait(pe, x1t_ready[c], s.n - 1)
                for k in range(TC):
                    ins = turn(b_t[c][:, k * P:(k + 1) * P], xn[:, s.u, c * TC + k, 0:D], ident[:])
                ins.then_inc(x_turned[c], 1)

            def make_k(s, c):
                pe.wait_ge(xt_ready[c], s.n + 1)
                wait(pe, phik_ready, s.n * CH + c)
                plus_one(b_k)
                for k in range(TC):
                    ins = mm(b_k[:, k * P:(k + 1) * P], xt[:, c, k * P:(k + 1) * P], w_t[:, 1, :],
                             start=False, stop=(k == TC - 1))
                ins.then_inc(k_made, 1)

            def make_q(s, c):
                pe.wait_ge(xt_ready[c], s.n + 1)
                wait(pe, phiq_ready, s.n * CH + c)
                plus_one(b_q)
                mm(b_q[:], w_t[:, 0, :], xt[:, c, :], start=False, stop=True).then_inc(q_made, 1)

            def make_g(s, c):
                pe.wait_ge(phik_ready, s.n * CH + (c + 1))
                if c == 0:
                    wait(pe, kvn_ready, s.n)
                for k in range(TC):
                    ins = mm(b_g[:, 0:D + 1], phik[:, c, k * P:(k + 1) * P], xn[:, s.u, c * TC + k, :],
                             start=(c == 0 and k == 0), stop=(c == 1 and k == TC - 1))
                ins.then_inc(g_made if c else g_half, 1)

            def turn_g(s):
                pe.wait_ge(g_kept, s.n + 1)
                turn(b_g[:, GT0:GT0 + P], g_sb[:, 0:D], ident[:]).then_inc(g_turned, 1)

            def make_kv(s):
                pe.wait_ge(gt_kept, s.n + 1)
                mm(b_g[:, KV0:KV0 + P], gt_sb[:], w_t[:, 2, :], start=True, stop=True).then_inc(kv_made, 1)

            def make_o(s, c):
                if c == 0:
                    pe.wait_ge(kvn_ready, s.n + 1)
                pe.wait_ge(phiq_ready, s.n * CH + (c + 1))
                wait(pe, o_ready, s.n * CH + c)
                for k in range(TC):
                    ins = mm(o_bank[k // 2][:, (k % 2) * 256:(k % 2) * 256 + ON],
                             phiqt[:, s.u, c, k * P:(k + 1) * P], kvn[:], start=True, stop=True)
                ins.then_inc(o_made, 1)

            def turn_o(s, c):
                pe.wait_ge(o_ready, s.n * CH + (c + 1))
                wait(pe, xt_ready[c], s.n + 2, NB)
                wait(pe, x1t_ready[c], s.n)
                for k in range(TC):
                    ins = turn(b_t[c][:, k * P:(k + 1) * P], on[:, c, k * P:(k + 1) * P], ident[:])
                ins.then_inc(o_turned[c], 1)

            def make_y(s, c):
                pe.wait_ge(ot_ready[c], s.n + 1)
                if c == 0:
                    wait(pe, places_read, s.n)
                else:
                    pe.wait_ge(x1_ready, s.n * CH + 1)
                for k in range(TC):
                    ins = mm(b_y[:, k * P:(k + 1) * P], ot[:, c, k * P:(k + 1) * P], w_t[:, 3, :],
                             start=True, stop=True)
                ins.then_inc(y_made, 1)

            def turn_x1(s, c):
                pe.wait_ge(x1_ready, s.n * CH + (c + 1))
                wait(pe, ot_ready[c], s.n + 1)
                for k in range(TC):
                    ins = turn(b_t[c][:, k * P:(k + 1) * P], x1[:, s.u, c * TC + k, :], ident[:])
                ins.then_inc(x1_turned[c], 1)

            def route(s, c):
                pe.wait_ge(x1t_ready[c], s.n + 1)
                if c == 0:
                    pe.wait_ge(x1_ready, s.n * CH + CH)
                    pe.wait_ge(wr_sum_kept, 1)
                for k in range(TC):
                    j = c * TC + k
                    ins = mm(b_y[:, j * E:(j + 1) * E], x1t[:, c, k * P:(k + 1) * P], wr_t[:],
                             start=True, stop=True)
                if c == 1:
                    ins.then_inc(logits_made, 1)

            def positions(s):
                pe.wait_ge(mask_ready, s.n + 1)
                pos = b_y[:, POS0:2 * POS0].rearrange("p (t e) -> p t e", e=E)
                mm(pos, ones_bf[:], seen_bf[:].rearrange("p (a e) -> p a e", a=1).to_broadcast([P, TILES, E]),
                   start=True, stop=False)
                for j in range(TILES):
                    m = mask_bf[:, j:j + 1, :]
                    if j < TILES - 1:
                        mm(pos[:, j + 1:, :], ident_bf[:], m.to_broadcast([P, TILES - 1 - j, E]),
                           start=False, stop=False)
                    ins = mm(pos, before[:], m.to_broadcast([P, TILES, E]), start=False, stop=(j == TILES - 1))
                ins.then_inc(pos_made, 1)

            def step(do):
                do(turn_o, 1, 0)
                do(positions, 2)
                do(make_q, 0, 0)
                do(turn_x, 0, 1)
                do(make_g, 0, 0)
                do(make_y, 1, 0)
                do(make_k, 0, 1)
                do(turn_o, 1, 1)
                do(make_q, 0, 1)
                do(make_y, 1, 1)
                do(turn_x1, 1, 0)
                do(make_g, 0, 1)
                do(turn_g, 0)
                do(turn_x1, 1, 1)
                do(make_kv, 0)
                do(make_o, 0, 0)
                do(route, 1, 0)
                do(route, 1, 1)
                do(turn_x, -1, 0)
                do(make_o, 0, 1)
                do(make_k, -1, 0)

            pe.wait_ge(w_kept, 1)
            mm(b_y[:, 0:E], ones_f[:], wr_t[:], start=True, stop=True).then_inc(wr_summed, 1)
            run(pe, step, -1, NB + 1, (3, 7))

            pe.wait_ge(spots_ready, NB)

            def products(out, weights, moving):
                terms = [(w[a], x[b]) for w, x in zip(weights, moving) for a, b in ((0, 0), (0, 1), (1, 0))]
                for j, (w, x) in enumerate(terms):
                    ins = mm(out, w, x, start=(j == 0), stop=(j == len(terms) - 1))
                return ins

            def turn_rows(e, m):
                c, v = chunk(e, m)
                if m == 0:
                    pe.wait_ge(rows_in[e.u], (e.half + 1) * ON_QUEUE)
                wait(pe, rt_lo_ready, c - 1)
                for k in range(PAIR):
                    ins = turn(bank[v][:, k * P:(k + 1) * P], rows[:, e.u, m * PAIR + k, 0:D], ident[:])
                ins.then_inc(r_turned, 1)

            def hidden(e, m):
                c, v = chunk(e, m)
                if m == 0:
                    pe.wait_ge(w_lo_ready, e.n + 1)
                pe.wait_ge(rt_lo_ready, c + 1)
                for i in range(IB):
                    ins = products(bank[2 + 2 * v + i // 2][:, (i % 2) * 256:(i % 2) * 256 + PAIR * P],
                                   [[w[:, e.u, i * P:(i + 1) * P] for w in w1_hl]], [[r[:, v, :] for r in rt_hl]])
                    if i % 2:
                        ins.then_inc(h_made, 1)

            def expert_out(e, m):
                c, v = chunk(e, m)
                pe.wait_ge(h_lo_ready, c * 2 + 2)
                wait(pe, yo_ready, c - 1)
                products(bank[6 + v][:, 0:PAIR * P],
                         [[w[:, e.u, i, :] for w in w2_hl] for i in range(IB)],
                         [[h[:, v, i, :] for h in hid_hl] for i in range(IB)]).then_inc(e_made, 1)

            def turn_y(e, m):
                c, v = chunk(e, m)
                pe.wait_ge(yt_ready, c + 1)
                for k in range(PAIR):
                    ins = turn(bank[6 + v][:, 256 + k * P:256 + (k + 1) * P], yt[:, v, k * P:(k + 1) * P], ident[:])
                ins.then_inc(y_turned, 1)

            run_experts(pe, lambda before, e, after: walk(
                before, e, after, lambda e: None, turn_rows, hidden, expert_out, turn_y))

        @block.scalar
        def _(act):
            f = nc.scalar.activation

            def first_norm(s, c):
                if c == 0:
                    act.wait_ge(ln_ready, s.n + 1)
                    wait(act, g_made, s.n - 1)
                for j in range(c * TC, (c + 1) * TC):
                    ins = f(xn[:, s.u, j, 0:D], xs[:, s.n, j, :], ACT.Identity,
                            bias=ln[:, s.u, 9, TILES + j:TILES + j + 1], scale=ln[:, s.u, 8, TILES + j:TILES + j + 1])
                ins.then_inc(xn_ready, 1)

            def keep_xt(s, c):
                act.wait_ge(x_turned[c], s.n + 1)
                wait(act, q_made, (s.n - 1) * CH + (c + 1))
                nc.scalar.copy(xt[:, c, :], b_t[c][:]).then_inc(xt_ready[c], 1)

            def exp_k(s, c):
                act.wait_ge(k_made, s.n * CH + (c + 1))
                wait(act, phik_ready, (s.n - 1) * CH + (c + 1))
                f(kx[:, c, :], b_k[:], ACT.Exp, bias=minus_one[:]).then_inc(k_exp, 1)

            def exp_q(s, c):
                act.wait_ge(q_made, s.n * CH + (c + 1))
                wait(act, phiq_ready, (s.n - 1) * CH + (c + 1))
                f(qx[:, c, :], b_q[:], ACT.Exp, bias=minus_one[:]).then_inc(q_exp, 1)

            def keep_g(s):
                act.wait_ge(g_made, s.n + 1)
                wait(act, kvn_ready, s.n)
                nc.scalar.copy(g_sb[:], b_g[:, 0:D + 1]).then_inc(g_kept, 1)

            def keep_gt(s):
                act.wait_ge(g_turned, s.n + 1)
                nc.scalar.copy(gt_sb[:], b_g[:, GT0:GT0 + P]).then_inc(gt_kept, 1)

            def keep_ot(s, c):
                act.wait_ge(o_turned[c], s.n + 1)
                wait(act, y_made, (s.n - 1) * CH + (c + 1))
                nc.scalar.copy(ot[:, c, :], b_t[c][:]).then_inc(ot_ready[c], 1)

            def rough_root(s):
                act.wait_ge(var_ready, s.n + (AHEAD + 1))
                f(ln[:, s.u, 5, :], ln[:, s.u, 4, :], ACT.Ln).then_inc(log_ready, 1)
                act.wait_ge(log_ready, s.n + (AHEAD + 1))
                f(ln[:, s.u, 6, :], ln[:, s.u, 5, :], ACT.Exp, scale=-0.5).then_inc(root_ready, 1)

            def keep_x1t(s, c):
                act.wait_ge(x1_turned[c], s.n + 1)
                wait(act, logits_made, s.n)
                nc.scalar.copy(x1t[:, c, :], b_t[c][:]).then_inc(x1t_ready[c], 1)

            def payload(s, c):
                if c == 0:
                    act.wait_ge(ln_ready, s.n + (AHEAD + 1))
                    wait(act, sent[s.u], s.half * (TILES * TOP * ON_QUEUE))
                for j in range(c * TC, (c + 1) * TC):
                    ins = f(pay[:, s.u, j, 0:D], x1[:, s.u, j, :], ACT.Identity,
                            bias=ln[:, s.u, 9, j:j + 1], scale=ln[:, s.u, 8, j:j + 1])
                    if j == 0:
                        ins.then_inc(pay_free, 1)
                if c == CH - 1:
                    ins.then_inc(pay_x, 1)

            def exp_logits(s):
                act.wait_ge(shifted, s.n + 1)
                f(expo[:], expo[:], ACT.Exp).then_inc(exps, 1)

            def step(do):
                do(payload, 3, 1)
                do(exp_q, 1, 0)
                do(keep_xt, 1, 1)
                do(keep_ot, 2, 1)
                do(exp_k, 1, 1)
                do(exp_q, 1, 1)
                do(keep_g, 1)
                do(keep_gt, 1)
                do(rough_root, 2, first=-AHEAD)
                do(keep_x1t, 2, 0)
                do(keep_x1t, 2, 1)
                do(first_norm, 0, 0)
                do(payload, 2, 0)
                do(keep_xt, 0, 0)
                do(exp_logits, 2)
                do(first_norm, 0, 1)
                do(exp_k, 0, 0)
                do(keep_ot, 1, 0)

            nc.scalar.preload_act_table_set("natural_log_exp_and_others")
            act.wait_ge(ones_set, 1)
            run(act, step, 0, NB + 2, (4, 8))

            def split_weights(e):
                wait(act, e_made, (e.n - 1) * NCH)
                act.wait_ge(w1_in[e.u], (e.half + 1) * ON_QUEUE)
                act.wait_ge(w2_in[e.u], (e.half + 1) * ON_QUEUE)
                nc.scalar.copy(w1_hl[0][:, e.u], w1[:, e.u])
                nc.scalar.copy(w2_hl[0][:, e.u].rearrange("p i d -> p (i d)"),
                               w2[:, e.u].rearrange("p i d -> p (i d)")).then_inc(w_hi_ready, 1)

            def split_rows(e, m):
                c, v = chunk(e, m)
                act.wait_ge(r_turned, c + 1)
                wait(act, h_made, c * 2 - 2)
                nc.scalar.copy(rt_hl[0][:, v, :], bank[v][:, 0:PAIR * P]).then_inc(rt_hi_ready, 1)

            def relu(e, m):
                c, v = chunk(e, m)
                for h in range(2):
                    act.wait_ge(h_made, c * 2 + h + 1)
                    if h == 0:
                        wait(act, e_made, c - 1)
                    f(hid_hl[0][:, v, 2 * h:2 * h + 2, :].rearrange("p i n -> p (i n)"), bank[2 + 2 * v + h][:],
                      ACT.Relu).then_inc(h_hi_ready, 1)

            def keep_yt(e, m):
                c, v = chunk(e, m)
                act.wait_ge(e_made, c + 1)
                wait(act, y_turned, c - 1)
                nc.scalar.copy(yt[:, v, :], bank[6 + v][:, 0:PAIR * P]).then_inc(yt_ready, 1)

            run_experts(act, lambda before, e, after: walk(
                before, e, after, split_weights, split_rows, relu, keep_yt, lambda e, m: None))

        @block.vector
        def _(dve):
            v = nc.vector
            v.memset(empty[:], 0.0).then_inc(empty_set, 1)
            dve.wait_ge(empty_set, 1)
            v.memset(empty[:, :, D + E].bitcast(I32), NB * S).then_inc(empty_set, 1)
            v.memset(xn[:, :, :, D:D + 1], 1.0)
            v.memset(seen[:], 0.0)
            v.memset(stats[:], 0.0)
            v.memset(minus_one[:], -1.0)
            v.memset(seen_bf[:], 0.0).then_inc(ones_set, 1)
            spread_links = Chain(dve, spread_chain, 4, -AHEAD)
            newton_links = Chain(dve, newton_chain, 3, -AHEAD)
            o_links, offset_links, choose_links, weigh_links, place_links = (
                Chain(dve, c, n) for c, n in ((o_chain, 2 * CH), (offset_chain, 2), (choose_chain, 4),
                                              (weigh_chain, 4), (place_chain, 4)))

            def first_stats(s):
                dve.wait_ge(x_in[s.u], (s.half + 1) * ON_QUEUE)
                for k in range(TILES):
                    ins = v.bn_stats(stats[:, TILES + k, :], xs[:, s.n, k, :])
                ins.then_inc(stats1_ready, 1)

            def spread(s):
                wait(dve, xn_ready, (s.n + 1) * CH)
                wait(dve, pay_x, s.n - 1)
                wait(dve, stats1_ready, s.n + (AHEAD + 1), NB)
                wait(dve, stats2_ready, s.n + 1)
                r, ch = ln[:, s.u], spread_links
                ch.begin(s)
                ch.link(v.tensor_tensor(r[:, 3, :], stats[:, :, 2], stats[:, :, 5], ALU.add))
                v.tensor_tensor(r[:, 0, :], stats[:, :, 1], stats[:, :, 4], ALU.add)
                ch.link(v.tensor_tensor(r[:, 1, :], stats[:, :, 1], stats[:, :, 4], ALU.subtract))
                v.tensor_scalar(r[:, 2, :], r[:, 0, :], 0.5, None, ALU.mult)
                ch.link(v.tensor_tensor(r[:, 1, :], r[:, 1, :], r[:, 1, :], ALU.mult))
                ch.link(v.scalar_tensor_tensor(out=r[:, 3, :], in0=r[:, 1, :], scalar=D / 4.0, in1=r[:, 3, :],
                                               op0=ALU.mult, op1=ALU.add))
                ch.end()
                v.tensor_scalar(r[:, 4, :], r[:, 3, :], 1.0 / D, LN_EPS, ALU.mult, ALU.add).then_inc(var_ready, 1)

            def newton(s):
                dve.wait_ge(root_ready, s.n + (AHEAD + 1))
                r, ch = ln[:, s.u], newton_links
                ch.begin(s)
                ch.link(v.tensor_tensor(r[:, 7, :], r[:, 6, :], r[:, 6, :], ALU.mult))
                ch.link(v.scalar_tensor_tensor(out=r[:, 7, :], in0=r[:, 7, :], scalar=-0.5, in1=r[:, 4, :],
                                               op0=ALU.mult, op1=ALU.mult))
                ch.link(v.scalar_tensor_tensor(out=r[:, 8, :], in0=r[:, 7, :], scalar=1.5, in1=r[:, 6, :],
                                               op0=ALU.add, op1=ALU.mult))
                ch.end()
                v.scalar_tensor_tensor(out=r[:, 9, :], in0=r[:, 2, :], scalar=-1.0, in1=r[:, 8, :],
                                       op0=ALU.mult, op1=ALU.mult).then_inc(ln_ready, 1)

            def phi_k(s, c):
                dve.wait_ge(k_exp, s.n * CH + (c + 1))
                wait(dve, g_made if c else g_half, s.n)
                v.scalar_tensor_tensor(out=phik[:, c, :], in0=b_k[:], scalar=1.0, in1=kx[:, c, :],
                                       op0=ALU.max, op1=ALU.min).then_inc(phik_ready, 1)

            def phi_q(s, c):
                dve.wait_ge(q_exp, s.n * CH + (c + 1))
                wait(dve, o_made, (s.n - 1) * CH)
                v.scalar_tensor_tensor(out=phiqt[:, s.u, c, :], in0=b_q[:], scalar=1.0, in1=qx[:, c, :],
                                       op0=ALU.max, op1=ALU.min).then_inc(phiq_ready, 1)

            def mask_kv(s):
                dve.wait_ge(kv_made, s.n + 1)
                wait(dve, o_made, s.n * CH)
                v.tensor_tensor(kvn[:, 0:D], b_g[:, KV0:KV0 + P], head_mask[:].rearrange("p h j -> p (h j)"),
                                ALU.mult)
                v.tensor_scalar(kvn[:, D:ON], head_sel[:], g_sb[:, D:D + 1], None, ALU.mult).then_inc(kvn_ready, 1)

            def normalise_o(s, c):
                dve.wait_ge(o_made, s.n * CH + (c + 1))
                wait(dve, o_turned[c], s.n)
                ch = o_links
                if c == 0:
                    ch.begin(s)
                else:
                    ch.base, ch.j = s.n * ch.per, ch.per // 2
                for h in range(2):
                    src = o_bank[h][:].rearrange("p (k n) -> p k n", n=256)[:, :, D:ON]
                    ins = v.tensor_scalar(nrm[:, c, h * 2 * HEADS:(h + 1) * 2 * HEADS].rearrange("p (k n) -> p k n", k=2),
                                          src, NORM_MIN, None, ALU.max)
                ch.link(ins)
                ch.link(v.reciprocal(rnrm[:, c, :], nrm[:, c, :]))
                for h in range(2):
                    src = o_bank[h][:].rearrange("p (k n) -> p k n", n=256)[:, :, 0:D]
                    r = rnrm[:, c, h * 2 * HEADS:(h + 1) * 2 * HEADS].rearrange("p (k h a) -> p k h a", k=2, a=1)
                    ins = v.tensor_tensor(
                        on[:, c, h * 256:(h + 1) * 256].rearrange("p (k h j) -> p k h j", k=2, j=HD),
                        src.rearrange("p k (h j) -> p k h j", j=HD), r.to_broadcast([P, 2, HEADS, HD]), ALU.mult)
                ins.then_inc(o_ready, 1)

            def residual(s, c):
                dve.wait_ge(y_made, s.n * CH + (c + 1))
                if c == 0:
                    wait(dve, x1_stored[s.u], s.half * ON_QUEUE)
                    wait(dve, pay_x, s.n - 1)
                    wait(dve, x1_turned[1], s.n - 1)
                half = x1[:, s.u, c * TC:(c + 1) * TC, :]
                v.tensor_tensor(half, b_y[:].rearrange("p (t d) -> p t d", d=D),
                                xs[:, s.n, c * TC:(c + 1) * TC, :], ALU.add).then_inc(x1_ready, 1)
                dve.wait_ge(x1_ready, s.n * CH + (c + 1))
                for k in range(TC):
                    ins = v.bn_stats(stats[:, c * TC + k, :], half[:, k, :])
                if c == CH - 1:
                    ins.then_inc(stats2_ready, 1)

            def bcast_e(m):
                return m[:].rearrange("p (a e) -> p a e", a=1).to_broadcast([P, TILES, E])

            def wide(m):
                return m.rearrange("p (t a) -> p t a", a=1).to_broadcast([P, TILES, E])

            def router_offset(s):
                dve.wait_ge(ln_ready, s.n + (AHEAD + 1))
                offset_links.begin(s)
                offset_links.link(v.tensor_tensor(offset[:], wide(ln[:, s.u, 9, 0:TILES]), bcast_e(wr_sum), ALU.mult))
                offset_links.link(v.tensor_tensor(offset[:], offset[:], bcast_e(bias_e), ALU.add))
                offset_links.end()

            def choose(s):
                dve.wait_ge(logits_made, s.n + 1)
                ch = choose_links
                ch.begin(s)
                v.tensor_tensor(logit[:], b_y[:, 0:TILES * E].rearrange("p (t e) -> p t e", e=E),
                                wide(ln[:, s.u, 8, 0:TILES]), ALU.mult).then_inc(logits_kept, 1)
                dve.wait_ge(logits_kept, s.n + 1)
                ch.link(v.tensor_tensor(logit[:], logit[:], offset[:], ALU.add))
                v.tensor_copy(seen_bf[:], seen[:])
                for k in range(TILES):
                    ins = v.max(top_val[:, k, :], logit[:, k, :])
                ch.link(ins)
                v.tensor_tensor(expo[:], logit[:], top_val[:, :, 0:1].to_broadcast([P, TILES, E]),
                                ALU.subtract).then_inc(shifted, 1)
                for k in range(TILES):
                    ins = v.max_index(top_idx[:, k, :], top_val[:, k, :], logit[:, k, :])
                ch.link(ins)
                for k in range(TOP):
                    ins = v.tensor_tensor(chosen[:, k], number_e[:],
                                          top_idx[:, :, k:k + 1].to_broadcast([P, TILES, E]), ALU.is_equal)
                ch.link(ins)
                ch.end()
                v.tensor_tensor(either[:], chosen[:, 0], chosen[:, 1], ALU.add)

            def weigh(s):
                dve.wait_ge(exps, s.n + 1)
                ch = weigh_links
                ch.begin(s)
                ch.link(v.tensor_reduce(total[:, 0, :], expo[:], AX.X, ALU.add))
                ch.link(v.reciprocal(total[:, 1, :], total[:, 0, :]))
                ch.link(v.tensor_tensor(weight[:], expo[:], wide(total[:, 1, :]), ALU.mult))
                wait(dve, pos_made, s.n)
                v.scalar_tensor_tensor(out=mask_bf[:], in0=weight[:], scalar=0.0, in1=either[:],
                                       op0=ALU.is_gt, op1=ALU.mult).then_inc(mask_ready, 1)
                dve.wait_ge(pay_free, s.n + 1)
                v.tensor_scalar(pay[:, s.u, :, D + E].bitcast(I32), pay[:, s.u, :, D + E].bitcast(I32),
                                2 * S, None, ALU.add)
                v.tensor_copy(pay[:, s.u, :, D:D + E], weight[:])
                dve.wait_ge(mask_ready, s.n + 1)
                v.tensor_reduce(taken[:], mask_bf[:].rearrange("p t e -> p e t"), AX.X, ALU.add)
                ch.link(v.scalar_tensor_tensor(out=base_m[:], in0=mask_bf[:], scalar=-FAR, in1=base_e[:],
                                               op0=ALU.mult, op1=ALU.add))
                ch.end()

            def find_places(s):
                dve.wait_ge(pos_made, s.n + 1)
                ch = place_links
                ch.begin(s)
                pos = b_y[:, POS0:2 * POS0].rearrange("p (t e) -> p t e", e=E)
                v.tensor_tensor(seen[:], seen[:], taken[:], ALU.add)
                ch.link(v.tensor_scalar(over[:], pos, float(CAP), FAR, ALU.is_ge, ALU.mult))
                v.tensor_tensor(place[:], pos, base_m[:], ALU.add).then_inc(places_read, 1)
                dve.wait_ge(places_read, s.n + 1)
                ch.link(v.tensor_tensor(place[:], place[:], over[:], ALU.add))
                ch.link(v.tensor_tensor(
                    place_k[:].rearrange("p k t e -> p k (t e)"), chosen[:].rearrange("p k t e -> p k (t e)"),
                    place[:].rearrange("p (a t) e -> p a (t e)", a=1).to_broadcast([P, TOP, TILES * E]), ALU.mult))
                ch.link(v.tensor_reduce(choice[:], place_k[:], AX.X, ALU.add))
                ch.end()
                v.tensor_copy(spot[:, s.u], choice[:]).then_inc(spots_ready, 1)

            def step(do):
                do(mask_kv, 1)
                do(newton, 2, first=-AHEAD)
                do(router_offset, 2)
                do(normalise_o, 1, 0)
                do(choose, 2)
                do(weigh, 2)
                do(phi_k, 0, 0)
                do(find_places, 2)
                do(normalise_o, 1, 1)
                do(phi_q, 0, 0)
                do(residual, 1, 0)
                do(first_stats, -1)
                do(phi_k, 0, 1)
                do(residual, 1, 1)
                do(spread, 1, first=-AHEAD)
                do(phi_q, 0, 1)

            dve.wait_ge(w_turned, 1)
            v.tensor_copy(w_t[:].rearrange("p c d -> p (c d)"), b_t0[:])
            v.tensor_copy(wr_t[:], b_t1[:, 0:E])
            dve.wait_ge(const_done, 8)
            dve.wait_ge(wr_in, ON_QUEUE)
            dve.wait_ge(payload_ids, 2)
            dve.wait_ge(ones_set, 1)
            v.tensor_copy(ident_bf[:], ident[:]).then_inc(w_kept, 1)
            dve.wait_ge(wr_summed, 1)
            v.tensor_copy(wr_sum[:], b_y[:, 0:E]).then_inc(wr_sum_kept, 1)
            run(dve, step, -1, NB + 1, (3, 7))

            def low(out, x, hi):
                return v.tensor_tensor(out, x, hi.bitcast(F32), ALU.subtract)

            def split_weights(e):
                dve.wait_ge(w_hi_ready, e.n + 1)
                low(w1_hl[1][:, e.u], w1[:, e.u], w1_hl[0][:, e.u])
                low(w2_hl[1][:, e.u], w2[:, e.u], w2_hl[0][:, e.u]).then_inc(w_lo_ready, 1)

            def split_rows(e, m):
                c, w = chunk(e, m)
                dve.wait_ge(rt_hi_ready, c + 1)
                low(rt_hl[1][:, w, :], bank[w][:, 0:PAIR * P], rt_hl[0][:, w, :]).then_inc(rt_lo_ready, 1)

            def relu(e, m):
                c, w = chunk(e, m)
                for h in range(2):
                    dve.wait_ge(h_hi_ready, c * 2 + h + 1)
                    hi, lo = (x[:, w, 2 * h:2 * h + 2, :].rearrange("p i n -> p (i n)") for x in hid_hl)
                    v.scalar_tensor_tensor(out=lo, in0=bank[2 + 2 * w + h][:], scalar=0.0, in1=hi.bitcast(F32),
                                           op0=ALU.max, op1=ALU.subtract).then_inc(h_lo_ready, 1)

            def weigh_out(e, m):
                c, w = chunk(e, m)
                dve.wait_ge(y_turned, c + 1)
                if m == 0:
                    wait(dve, added[e.u], e.half * (ET * ON_QUEUE))
                for k in range(PAIR):
                    j = m * PAIR + k
                    ins = v.tensor_scalar(yo[:, e.u, j, :], bank[6 + w][:, 256 + k * P:256 + (k + 1) * P],
                                          rows[:, e.u, j, bass.ds(e.n + D, 1)], None, ALU.mult)
                ins.then_inc(yo_ready, 1)

            run_experts(dve, lambda before, e, after: walk(
                before, e, after, split_weights, split_rows, relu, lambda e, m: None, weigh_out))


_INS = ["L0_attn_x", "L0_attn_w_qkv", "L0_attn_w_out", "L0_ffn_W_router", "L0_ffn_b_router",
        "L0_ffn_experts_inter", "L0_ffn_experts_out"]
_OUTS = [((8, 1024, 128), "float32")]


def kernel(**inputs):
    import numpy as _np
    import concourse.bacc as _bacc
    from concourse import mybir as _mybir
    from concourse.bass_utils import run_bass_kernel_spmd as _run

    nc = _bacc.Bacc("TRN2", target_bir_lowering=False, num_devices=1)
    arrays, args = {}, []
    for name in _INS:
        a = _np.ascontiguousarray(inputs[name])
        arrays[f"in_{name}_dram"] = a
        args.append(nc.dram_tensor(f"in_{name}_dram", a.shape, _mybir.dt.from_np(a.dtype), kind="ExternalInput").ap())
    for i, (shape, dtype) in enumerate(_OUTS):
        dt = _mybir.dt.from_np(_np.dtype(dtype))
        args.append(nc.dram_tensor(f"out_{i}_dram", shape, dt, kind="ExternalOutput").ap())
    moe_layer(nc, *args)
    r = _run(nc, [arrays], core_ids=[0])
    got = tuple(r.results[0][f"out_{i}_dram"] for i in range(len(_OUTS)))
    return got[0]
```

```python
from contextlib import ExitStack

import concourse.bass as bass
from concourse import mybir

F32 = mybir.dt.float32
F32R = mybir.dt.float32r
BF16 = mybir.dt.bfloat16
I32 = mybir.dt.int32
U32 = mybir.dt.uint32
ALU = mybir.AluOpType
ACT = mybir.ActivationFunctionType
AX = mybir.AxisListType

P = 128
HEADS = 16
TOP = 2
LN_EPS = 1e-5
NORM_MIN = 1e-6
ON_QUEUE = 16
WARM_UP = 20
FAR = 16384.0


class Seq:

    def __init__(self, n, parity, half):
        self.n, self.u, self.half = n, parity, half

    @staticmethod
    def fixed(n):
        return Seq(n, n % 2, n // 2)

    def shift(self, k):
        if isinstance(self.n, int):
            return Seq.fixed(self.n + k)
        v = self.u + k
        return Seq(self.n + k, v % 2, self.half + v // 2)


def wait(eng, sem, value, most=None):
    if isinstance(value, int):
        if most is not None:
            value = min(value, most)
        if value <= 0:
            return
    eng.wait_ge(sem, value)


class Chain:

    def __init__(self, eng, sem, per, first=0):
        self.eng, self.sem, self.per, self.first = eng, sem, per, first

    def begin(self, b, done=0):
        self.base, self.j = (b.n - self.first) * self.per, done

    def tick(self, ins):
        self.j += 1
        assert self.j <= self.per
        ins.then_inc(self.sem, 1)
        return self.j

    def after(self, j):
        self.eng.wait_ge(self.sem, self.base + j)

    def link(self, ins):
        self.after(self.tick(ins))

    def end(self):
        assert self.j == self.per, (self.j, self.per)


def moe_layer(nc, x, w_qkv, w_out, w_router, b_router, w_inter, w_exp_out, out):
    NB, S, D = x.shape
    E, _, I = w_inter.shape
    TILES = S // P
    CH = 2
    TC = TILES // CH
    HD = D // HEADS
    CAP = -(-NB * S * 5 // (E * 4))
    ET = CAP // P
    PAIR = 2
    NCH = ET // PAIR
    IB = I // P
    PAY = D + E + 1
    ON = D + HEADS
    AHEAD = 2
    assert D == P and CAP % P == 0 and ET % PAIR == 0 and TC * P == 512

    x_v = x.rearrange("b (p t) d -> b p (t d)", p=P)
    out_v = out.rearrange("b (p t) d -> b p (t d)", p=P)
    out_rows = out.rearrange("b s d -> (b s) d")
    places = nc.dram_tensor("places", [E * CAP, PAY], F32).ap()
    places_v = places.rearrange("(e p t) c -> e p (t c)", e=E, p=P)
    w2_v = w_exp_out.rearrange("e (c p) h -> e p c h", p=P)

    with ExitStack() as ctx:
        def sb(name, shape, dt=F32):
            return ctx.enter_context(nc.sbuf_tensor(name, shape, dt))

        def sem(name):
            return ctx.enter_context(nc.semaphore(name))

        bank = [ctx.enter_context(nc.psum_tensor(f"bank{i}", [P, 512], F32)) for i in range(8)]

        ident = sb("ident", [P, P])
        ident_bf = sb("ident_bf", [P, P], BF16)
        before = sb("before", [P, P], BF16)
        ones_bf = sb("ones_bf", [P, P], BF16)
        head_mask = sb("head_mask", [P, HEADS, HD])
        head_sel = sb("head_sel", [P, HEADS])
        number_e = sb("number_e", [P, TILES, E])
        base_e = sb("base_e", [P, TILES, E])
        bias_e = sb("bias_e", [P, E])
        w_raw = sb("w_raw", [P, 4, P])
        wr_raw = sb("wr_raw", [E, P])
        w_t = sb("w_t", [P, 4, P])
        wr_raw_t = sb("wr_raw_t", [P, E])
        wr_t = sb("wr_t", [P, E])
        ones_f = sb("ones_f", [P, P])
        minus_one = sb("minus_one", [P, 1])
        empty = sb("empty", [P, ET, PAY])
        xs = sb("xs", [P, NB, TILES, D])
        stats = sb("stats", [P, AHEAD + NB, 2 * TILES, 6])
        ln = sb("ln", [P, 2, 10, 2 * TILES])
        xn = sb("xn", [P, 2, TILES, D + 1])
        xt = sb("xt", [P, CH, 512])
        kx = sb("kx", [P, CH, 512])
        qx = sb("qx", [P, CH, 512])
        phik = sb("phik", [P, CH, 512])
        phiqt = sb("phiqt", [P, 2, CH, 512])
        g_sb = sb("g_sb", [P, D + 1])
        gt_sb = sb("gt_sb", [P, D])
        kvn = sb("kvn", [P, ON])
        nrm = sb("nrm", [P, CH, TC * HEADS])
        rnrm = sb("rnrm", [P, CH, TC * HEADS])
        on = sb("on", [P, CH, 512])
        ot = sb("ot", [P, CH, 512])
        x1 = sb("x1", [P, 2, TILES, D])
        pay = sb("pay", [P, 2, TILES, PAY])
        x1t = sb("x1t", [P, CH, 512])
        logit = sb("logit", [P, TILES, E])
        top_val = sb("top_val", [P, TILES, 8])
        top_idx = sb("top_idx", [P, TILES, 8], U32)
        expo = sb("expo", [P, TILES, E])
        total = sb("total", [P, 2, TILES])
        chosen = sb("chosen", [P, TOP, TILES, E])
        either = sb("either", [P, TILES, E])
        taken = sb("taken", [P, E])
        base_m = sb("base_m", [P, TILES, E])
        over = sb("over", [P, TILES, E])
        place = sb("place", [P, TILES, E])
        place_k = sb("place_k", [P, TOP, TILES, E])
        mask_bf = sb("mask_bf", [P, TILES, E], BF16)
        seen = sb("seen", [P, E], BF16)
        choice = sb("choice", [P, TOP, TILES])
        spot = sb("spot", [P, 2, TOP, TILES], I32)
        rows = sb("rows", [P, 2, ET, PAY])
        w1 = sb("w1", [P, 2, I])
        w2 = sb("w2", [P, 2, IB, D])
        w1_hl = [sb(f"w1_{h}", [P, 2, I], F32R) for h in ("hi", "lo")]
        w2_hl = [sb(f"w2_{h}", [P, 2, IB, D], F32R) for h in ("hi", "lo")]
        rt_hl = [sb(f"rt_{h}", [P, 2, PAIR * P], F32R) for h in ("hi", "lo")]
        hid_hl = [sb(f"hid_{h}", [P, 2, IB, PAIR * P], F32R) for h in ("hi", "lo")]
        yt = sb("yt", [P, 2, PAIR * P])
        row_weights = sb("row_weights", [P, 2, ET, E])
        row_tokens = sb("row_tokens", [P, 2, ET], I32)
        yo = sb("yo", [P, 2, ET, D])

        w_in, wr_in = sem("w_in"), sem("wr_in")
        x_in = [sem(f"x_in{u}") for u in range(2)]
        const_z, const_done, payload_ids = sem("const_z"), sem("const_done"), sem("payload_ids")
        empty_set, empty_stored = sem("empty_set"), sem("empty_stored")
        filled = sem("filled")
        wr_summed, wr_centred = sem("wr_summed"), sem("wr_centred")
        w_turned, w_kept = sem("w_turned"), sem("w_kept")
        spread_chain, newton_chain, var_ready, log_ready, root_ready, ln_ready, xn_ready = (
            sem(s) for s in ("spread_chain", "newton_chain", "var_ready", "log_ready", "root_ready", "ln_ready",
                             "xn_ready"))
        stats1_ready, stats2_ready = sem("stats1_ready"), sem("stats2_ready")
        x_turned = [sem(f"x_turned{c}") for c in range(CH)]
        xt_ready = [sem(f"xt_ready{c}") for c in range(CH)]
        k_made, q_made = sem("k_made"), sem("q_made")
        k_exp, q_exp = sem("k_exp"), sem("q_exp")
        phik_ready, phiq_ready = sem("phik_ready"), sem("phiq_ready")
        g_half, g_made, g_kept, g_turned, gt_kept, kv_made, kvn_ready = (
            sem(s) for s in ("g_half", "g_made", "g_kept", "g_turned", "gt_kept", "kv_made", "kvn_ready"))
        o_made, o_chain, o_ready = sem("o_made"), sem("o_chain"), sem("o_ready")
        o_turned = [sem(f"o_turned{c}") for c in range(CH)]
        ot_ready = [sem(f"ot_ready{c}") for c in range(CH)]
        y_made, x1_ready = sem("y_made"), sem("x1_ready")
        x1_stored = [sem(f"x1_stored{u}") for u in range(2)]
        x1_turned = [sem(f"x1_turned{c}") for c in range(CH)]
        x1t_ready = [sem(f"x1t_ready{c}") for c in range(CH)]
        logits_made, logits_kept, shifted, exps, mask_ready, pay_x, places_read = (
            sem(s) for s in ("logits_made", "logits_kept", "shifted", "exps", "mask_ready", "pay_x",
                             "places_read"))
        choose_chain, weigh_chain, place_chain = (
            sem(s) for s in ("choose_chain", "weigh_chain", "place_chain"))
        pool_going = sem("pool_going")
        pos_made, spots_ready = sem("pos_made"), sem("spots_ready")
        sent = [sem(f"sent{u}") for u in range(2)]
        first_rows_in = [sem(f"first_rows_in{u}") for u in range(2)]
        rows_in = [sem(f"rows_in{u}") for u in range(2)]
        w1_in = [sem(f"w1_in{u}") for u in range(2)]
        w2_in = [sem(f"w2_in{u}") for u in range(2)]
        tags_kept = sem("tags_kept")
        w_hi_ready, w_lo_ready, r_turned, rt_hi_ready, rt_lo_ready = (
            sem(s) for s in ("w_hi_ready", "w_lo_ready", "r_turned", "rt_hi_ready", "rt_lo_ready"))
        h_made, h_hi_ready, h_lo_ready, e_made, yt_ready, y_turned, yo_ready = (
            sem(s) for s in ("h_made", "h_hi_ready", "h_lo_ready", "e_made", "yt_ready", "y_turned", "yo_ready"))
        added = [sem(f"added{u}") for u in range(2)]

        b_t0, b_t1, b_k, b_q, b_g, b_o0, b_o1, b_y = bank
        o_bank = [b_o0, b_o1]
        b_t = [b_t0, b_t1]
        GT0, KV0 = 160, 320
        POS0 = TILES * E

        def run(eng, step, first, last, loop):
            def doer(b, t, last_t):
                def do(work, k, *part, first=0):
                    if t - k >= first and last_t - k < NB:
                        work(b.shift(-k), *part)
                return do

            for t in range(first, loop[0]):
                step(doer(Seq.fixed(t), t, t), t)
            with eng.Fori(0, (loop[1] - loop[0]) // 2) as i:
                for t in range(loop[0], loop[0] + 2):
                    step(doer(Seq(i * 2 + t, t % 2, i + t // 2), t, loop[1] - 2 + (t - loop[0])), t)
            for t in range(loop[1], last + 1):
                step(doer(Seq.fixed(t), t, t), t)

        def run_experts(eng, expert):
            def fixed(n):
                return Seq.fixed(n) if 0 <= n < E else None

            for n in (0, 1):
                expert(fixed(n - 1), fixed(n), fixed(n + 1))
            with eng.Fori(1, E // 2 - 1) as i:
                for u in range(2):
                    e = Seq(i * 2 + u, u, i)
                    expert(e.shift(-1), e, e.shift(1))
            for n in (E - 2, E - 1):
                expert(fixed(n - 1), fixed(n), fixed(n + 1))

        def walk(before, e, after, split, rows, hidden, late, last):
            chunks = {m: (e, m) for m in range(NCH)}
            for k in (1, 2):
                if before:
                    chunks[-k] = (before, NCH - k)
            if after:
                chunks[NCH] = (after, 0)
            if not before:
                split(e)
                rows(e, 0)
            for m in range(NCH):
                if m + 1 in chunks:
                    rows(*chunks[m + 1])
                hidden(e, m)
                if m - 2 in chunks:
                    last(*chunks[m - 2])
                if m - 1 in chunks:
                    late(*chunks[m - 1])
                if m == 1 and after:
                    split(after)
            if not after:
                last(*chunks[NCH - 2])
                late(e, NCH - 1)
                last(e, NCH - 1)

        def chunk(e, m):
            return e.n * NCH + m, (e.u * NCH + m) % 2

        block = ctx.enter_context(nc.Block())

        @block.sync
        def _(sp):
            def load_x(b):
                wait(sp, x_in[b.u], b.half * ON_QUEUE)
                sp.dma_start(xs[:, b.n].rearrange("p t d -> p (t d)"), x_v[b.n]).then_inc(x_in[b.u], ON_QUEUE)

            load_x(Seq.fixed(0))
            sp.dma_start(w_raw[:, 0:3, :], w_qkv.rearrange("(c p) d -> p c d", p=P)).then_inc(w_in, ON_QUEUE)
            sp.dma_start(w_raw[:, 3, :], w_out).then_inc(w_in, ON_QUEUE)
            sp.dma_start(wr_raw[:], w_router).then_inc(w_in, ON_QUEUE)
            sp.dma_start(bias_e[:], b_router.rearrange("(a e) -> a e", a=1).to_broadcast([P, E])).then_inc(wr_in, ON_QUEUE)
            load_x(Seq.fixed(1))
            with sp.Fori(1, NB // 2) as i:
                for u in range(2):
                    load_x(Seq(i * 2 + u, u, i))
            sp.wait_ge(empty_set, 2)
            for e in range(E):
                sp.dma_start(places_v[e], empty[:].rearrange("p t c -> p (t c)")).then_inc(empty_stored, ON_QUEUE)

            def load_weights(e):
                wait(sp, w_lo_ready, (e.half - 1) * 2 + (e.u + 1))
                sp.dma_start(w1[:, e.u], w_inter[e.n]).then_inc(w1_in[e.u], ON_QUEUE)
                sp.dma_start(w2[:, e.u], w2_v[e.n]).then_inc(w2_in[e.u], ON_QUEUE)

            def load_rows(e):
                wait(sp, r_turned, (e.half - 1) * (2 * NCH) + (e.u + 1) * NCH)
                wait(sp, tags_kept, (e.half - 1) * 2 + (e.u + 1))
                for tiles, arrived in ((slice(0, PAIR), first_rows_in), (slice(PAIR, ET), rows_in)):
                    sp.dma_start(rows[:, e.u, tiles].rearrange("p t c -> p (t c)"),
                                 places_v[e.n][:, tiles.start * PAY:tiles.stop * PAY]).then_inc(arrived[e.u], ON_QUEUE)

            for u in range(2):
                load_weights(Seq.fixed(u))
            with sp.Fori(0, NB // 2) as i:
                for u in range(2):
                    sp.wait_ge(x1_ready, (i * 2 + u) * CH + CH)
                    sp.dma_start(out_v[i * 2 + u], x1[:, u].rearrange("p t d -> p (t d)")).then_inc(x1_stored[u], ON_QUEUE)
            for u in range(2):
                sp.wait_ge(sent[u], NB // 2 * TILES * TOP * ON_QUEUE)
            for u in range(2):
                load_rows(Seq.fixed(u))
            with sp.Fori(1, E // 2) as i:
                for u in range(2):
                    load_weights(Seq(i * 2 + u, u, i))
                    load_rows(Seq(i * 2 + u, u, i))

        @block.gpsimd
        def _(pool):
            g = nc.gpsimd
            g.memset(ident[:], 0.0).then_inc(const_z, 1)
            g.memset(before[:], 1.0).then_inc(const_z, 1)
            g.memset(head_mask[:], 1.0).then_inc(const_z, 1)
            g.memset(head_sel[:], 1.0).then_inc(const_z, 1)
            g.memset(ones_bf[:], 1.0).then_inc(const_done, 1)
            g.memset(ones_f[:], 1.0).then_inc(const_done, 1)
            pool.wait_ge(const_z, 4)
            g.affine_select(out=ident[:], in_=ident[:], compare_op=ALU.not_equal, fill=1.0, base=0,
                            pattern=[[-1, P]], channel_multiplier=1).then_inc(const_done, 1)
            g.affine_select(out=before[:], in_=before[:], compare_op=ALU.is_gt, fill=0.0, base=0,
                            pattern=[[1, P]], channel_multiplier=-1).then_inc(const_done, 1)
            g.affine_select(out=head_mask[:], in_=head_mask[:], compare_op=ALU.is_ge, fill=0.0, base=0,
                            pattern=[[-HD, HEADS], [0, HD]], channel_multiplier=1).then_inc(const_z, 1)
            g.affine_select(out=head_sel[:], in_=head_sel[:], compare_op=ALU.is_ge, fill=0.0, base=0,
                            pattern=[[-HD, HEADS]], channel_multiplier=1).then_inc(const_z, 1)
            pool.wait_ge(const_z, 6)
            g.affine_select(out=head_mask[:], in_=head_mask[:], compare_op=ALU.is_ge, fill=0.0, base=HD - 1,
                            pattern=[[HD, HEADS], [0, HD]], channel_multiplier=-1).then_inc(const_done, 1)
            g.affine_select(out=head_sel[:], in_=head_sel[:], compare_op=ALU.is_ge, fill=0.0, base=HD - 1,
                            pattern=[[HD, HEADS]], channel_multiplier=-1).then_inc(const_done, 1)
            g.iota(number_e[:], pattern=[[0, TILES], [1, E]], base=0, channel_multiplier=0,
                   allow_small_or_imprecise_dtypes=True).then_inc(const_done, 1)
            g.iota(base_e[:], pattern=[[0, TILES], [CAP, E]], base=int(FAR), channel_multiplier=0,
                   allow_small_or_imprecise_dtypes=True).then_inc(const_done, 1)
            for u in range(2):
                g.iota(pay[:, u, :, D + E].bitcast(I32), pattern=[[1, TILES]], base=(u - 2) * S,
                       channel_multiplier=TILES).then_inc(payload_ids, 1)

            def send(b):
                for t in range(TILES):
                    for k in range(TOP):
                        if t == 0 and k == 0:
                            pool.wait_ge(empty_stored, E * ON_QUEUE)
                            pool.wait_ge(pay_x, b.n + 1)
                            pool.wait_ge(spots_ready, b.n + 1)
                            pool.sem_inc(pool_going, 1)
                        g.indirect_dma_start(
                            out=places, out_offset=bass.IndirectOffsetOnAxis(ap=spot[:, b.u, k, t:t + 1], axis=0),
                            in_=pay[:, b.u, t, :], in_offset=None, bounds_check=E * CAP - 1,
                            oob_is_err=False).then_inc(sent[b.u], ON_QUEUE)

            with pool.Fori(0, NB // 2) as i:
                for u in range(2):
                    send(Seq(i * 2 + u, u, i))

            def add(before, e, after):
                if before:
                    pool.wait_ge(added[before.u], (before.half + 1) * (ET * ON_QUEUE))
                for m in range(NCH):
                    for stored in x1_stored:
                        pool.wait_ge(stored, NB // 2 * ON_QUEUE)
                    pool.wait_ge(yo_ready, e.n * NCH + (m + 1))
                    pool.sem_inc(pool_going, 1)
                    for k in range(PAIR):
                        t = m * PAIR + k
                        g.indirect_dma_start(
                            out=out_rows,
                            out_offset=bass.IndirectOffsetOnAxis(ap=row_tokens[:, e.u, t:t + 1], axis=0),
                            in_=yo[:, e.u, t, :], in_offset=None, bounds_check=NB * S - 1, oob_is_err=False,
                            compute_op=ALU.add).then_inc(added[e.u], ON_QUEUE)

            run_experts(pool, add)
            for u in range(2):
                pool.wait_ge(added[u], E // 2 * ET * ON_QUEUE)

        @block.tensor
        def _(pe):
            mm, turn = nc.tensor.matmul, nc.tensor.transpose
            pe.wait_ge(const_done, 8)
            pe.wait_ge(w_in, 3 * ON_QUEUE)
            for c in range(4):
                turn(b_t0[:, c * P:(c + 1) * P], w_raw[:, c, :], ident[:])
            turn(b_t1[:, 0:E], wr_raw[:], ident[0:E, 0:E]).then_inc(w_turned, 1)

            def plus_one(b_out):
                mm(b_out[:].rearrange("p (k n) -> p k n", n=P), ones_bf[0:1, :],
                   ones_bf[0:1, :].rearrange("p (a n) -> p a n", a=1).to_broadcast([1, TC, P]), start=True, stop=False)

            def turn_x(s, c):
                pe.wait_ge(xn_ready, s.n * CH + (c + 1))
                wait(pe, x1t_ready[c], s.n - 1)
                for k in range(TC):
                    ins = turn(b_t[c][:, k * P:(k + 1) * P], xn[:, s.u, c * TC + k, 0:D], ident[:])
                ins.then_inc(x_turned[c], 1)

            def make_k(s, c):
                pe.wait_ge(xt_ready[c], s.n + 1)
                wait(pe, phik_ready, s.n * CH + c)
                plus_one(b_k)
                for k in range(TC):
                    ins = mm(b_k[:, k * P:(k + 1) * P], xt[:, c, k * P:(k + 1) * P], w_t[:, 1, :],
                             start=False, stop=(k == TC - 1))
                ins.then_inc(k_made, 1)

            def make_q(s, c):
                pe.wait_ge(xt_ready[c], s.n + 1)
                wait(pe, phiq_ready, s.n * CH + c)
                plus_one(b_q)
                mm(b_q[:], w_t[:, 0, :], xt[:, c, :], start=False, stop=True).then_inc(q_made, 1)

            def make_g(s, c):
                pe.wait_ge(phik_ready, s.n * CH + (c + 1))
                if c == 0:
                    wait(pe, kvn_ready, s.n)
                for k in range(TC):
                    ins = mm(b_g[:, 0:D + 1], phik[:, c, k * P:(k + 1) * P], xn[:, s.u, c * TC + k, :],
                             start=(c == 0 and k == 0), stop=(c == 1 and k == TC - 1))
                ins.then_inc(g_made if c else g_half, 1)

            def turn_g(s):
                pe.wait_ge(g_kept, s.n + 1)
                turn(b_g[:, GT0:GT0 + P], g_sb[:, 0:D], ident[:]).then_inc(g_turned, 1)

            def make_kv(s):
                pe.wait_ge(gt_kept, s.n + 1)
                mm(b_g[:, KV0:KV0 + P], gt_sb[:], w_t[:, 2, :], start=True, stop=True).then_inc(kv_made, 1)

            def make_o(s, c):
                if c == 0:
                    pe.wait_ge(kvn_ready, s.n + 1)
                pe.wait_ge(phiq_ready, s.n * CH + (c + 1))
                wait(pe, o_ready, s.n * CH + c)
                for k in range(TC):
                    ins = mm(o_bank[k // 2][:, (k % 2) * 256:(k % 2) * 256 + ON],
                             phiqt[:, s.u, c, k * P:(k + 1) * P], kvn[:], start=True, stop=True)
                ins.then_inc(o_made, 1)

            def turn_o(s, c):
                pe.wait_ge(o_ready, s.n * CH + (c + 1))
                wait(pe, xt_ready[c], s.n + 2, NB)
                wait(pe, x1t_ready[c], s.n)
                for k in range(TC):
                    ins = turn(b_t[c][:, k * P:(k + 1) * P], on[:, c, k * P:(k + 1) * P], ident[:])
                ins.then_inc(o_turned[c], 1)

            def make_y(s, c):
                pe.wait_ge(ot_ready[c], s.n + 1)
                if c == 0:
                    wait(pe, places_read, s.n)
                else:
                    pe.wait_ge(x1_ready, s.n * CH + 1)
                for k in range(TC):
                    ins = mm(b_y[:, k * P:(k + 1) * P], ot[:, c, k * P:(k + 1) * P], w_t[:, 3, :],
                             start=True, stop=True)
                ins.then_inc(y_made, 1)

            def turn_x1(s, c):
                pe.wait_ge(x1_ready, s.n * CH + (c + 1))
                wait(pe, ot_ready[c], s.n + 1)
                for k in range(TC):
                    ins = turn(b_t[c][:, k * P:(k + 1) * P], x1[:, s.u, c * TC + k, :], ident[:])
                ins.then_inc(x1_turned[c], 1)

            def route(s, c):
                pe.wait_ge(x1t_ready[c], s.n + 1)
                if c == 0:
                    pe.wait_ge(x1_ready, s.n * CH + CH)
                    pe.wait_ge(wr_centred, 1)
                for k in range(TC):
                    j = c * TC + k
                    ins = mm(b_y[:, j * E:(j + 1) * E], x1t[:, c, k * P:(k + 1) * P], wr_t[:],
                             start=True, stop=True)
                if c == 1:
                    ins.then_inc(logits_made, 1)

            def positions(s):
                pe.wait_ge(mask_ready, s.n + 1)
                pos = b_y[:, POS0:2 * POS0].rearrange("p (t e) -> p t e", e=E)
                mm(pos, ones_bf[:], seen[:].rearrange("p (a e) -> p a e", a=1).to_broadcast([P, TILES, E]),
                   start=True, stop=False)
                for j in range(TILES):
                    m = mask_bf[:, j:j + 1, :]
                    if j < TILES - 1:
                        mm(pos[:, j + 1:, :], ident_bf[:], m.to_broadcast([P, TILES - 1 - j, E]),
                           start=False, stop=False)
                    ins = mm(pos, before[:], m.to_broadcast([P, TILES, E]), start=False, stop=(j == TILES - 1))
                ins.then_inc(pos_made, 1)

            def step(do, t):
                do(turn_g, 1)
                do(turn_x1, 2, 1)
                do(route, 2, 0)
                do(make_kv, 1)
                do(route, 2, 1)
                do(make_o, 1, 0)
                do(turn_x, 0, 0)
                do(make_k, 0, 0)
                do(make_o, 1, 1)
                do(turn_x, 0, 1)
                do(turn_o, 1, 0)
                do(positions, 2)
                do(make_q, 0, 0)
                do(make_k, 0, 1)
                do(make_y, 1, 0)
                do(turn_o, 1, 1)
                do(make_g, 0, 0)
                do(make_y, 1, 1)
                do(make_q, 0, 1)
                do(make_g, 0, 1)
                do(turn_x1, 1, 0)

            pe.wait_ge(w_kept, 1)
            mm(b_y[:, 0:E], ones_f[:], wr_raw_t[:], start=True, stop=True).then_inc(wr_summed, 1)
            run(pe, step, 0, NB + 1, (4, 8))

            pe.wait_ge(spots_ready, NB)
            for u in range(2):
                pe.wait_ge(sent[u], NB // 2 * TILES * TOP * ON_QUEUE)
            for k in range(WARM_UP):
                turn(bank[2][:, 0:P], ident[:], ident[:])

            def products(out, weights, moving):
                terms = [(w[a], x[b]) for w, x in zip(weights, moving) for a, b in ((0, 0), (0, 1), (1, 0))]
                for j, (w, x) in enumerate(terms):
                    ins = mm(out, w, x, start=(j == 0), stop=(j == len(terms) - 1))
                return ins

            def turn_rows(e, m):
                c, v = chunk(e, m)
                if m <= 1:
                    pe.wait_ge((rows_in if m else first_rows_in)[e.u], (e.half + 1) * ON_QUEUE)
                wait(pe, rt_lo_ready, c - 1)
                for k in range(PAIR):
                    ins = turn(bank[v][:, k * P:(k + 1) * P], rows[:, e.u, m * PAIR + k, 0:D], ident[:])
                ins.then_inc(r_turned, 1)

            def hidden(e, m):
                c, v = chunk(e, m)
                if m == 0:
                    pe.wait_ge(w_lo_ready, e.n + 1)
                pe.wait_ge(rt_lo_ready, c + 1)
                for i in range(IB):
                    ins = products(bank[2 + 2 * v + i // 2][:, (i % 2) * 256:(i % 2) * 256 + PAIR * P],
                                   [[w[:, e.u, i * P:(i + 1) * P] for w in w1_hl]], [[r[:, v, :] for r in rt_hl]])
                    if i % 2:
                        ins.then_inc(h_made, 1)

            def expert_out(e, m):
                c, v = chunk(e, m)
                pe.wait_ge(h_lo_ready, c * 2 + 2)
                wait(pe, yo_ready, c - 1)
                products(bank[6 + v][:, 0:PAIR * P],
                         [[w[:, e.u, i, :] for w in w2_hl] for i in range(IB)],
                         [[h[:, v, i, :] for h in hid_hl] for i in range(IB)]).then_inc(e_made, 1)

            def turn_y(e, m):
                c, v = chunk(e, m)
                pe.wait_ge(yt_ready, c + 1)
                for k in range(PAIR):
                    ins = turn(bank[6 + v][:, 256 + k * P:256 + (k + 1) * P], yt[:, v, k * P:(k + 1) * P], ident[:])
                ins.then_inc(y_turned, 1)

            run_experts(pe, lambda before, e, after: walk(
                before, e, after, lambda e: None, turn_rows, hidden, expert_out, turn_y))

        @block.scalar
        def _(act):
            f = nc.scalar.activation

            def first_norm(s, c):
                if c == 0:
                    act.wait_ge(ln_ready, s.n + 1)
                    wait(act, g_made, s.n - 1)
                for j in range(c * TC, (c + 1) * TC):
                    ins = f(xn[:, s.u, j, 0:D], xs[:, s.n, j, :], ACT.Identity,
                            bias=ln[:, s.u, 9, TILES + j:TILES + j + 1], scale=ln[:, s.u, 8, TILES + j:TILES + j + 1])
                ins.then_inc(xn_ready, 1)

            def keep_xt(s, c):
                act.wait_ge(x_turned[c], s.n + 1)
                wait(act, q_made, (s.n - 1) * CH + (c + 1))
                nc.scalar.copy(xt[:, c, :], b_t[c][:]).then_inc(xt_ready[c], 1)

            def exp_k(s, c):
                act.wait_ge(k_made, s.n * CH + (c + 1))
                wait(act, phik_ready, (s.n - 1) * CH + (c + 1))
                f(kx[:, c, :], b_k[:], ACT.Exp, bias=minus_one[:]).then_inc(k_exp, 1)

            def exp_q(s, c):
                act.wait_ge(q_made, s.n * CH + (c + 1))
                wait(act, phiq_ready, (s.n - 1) * CH + (c + 1))
                f(qx[:, c, :], b_q[:], ACT.Exp, bias=minus_one[:]).then_inc(q_exp, 1)

            def keep_g(s):
                act.wait_ge(g_made, s.n + 1)
                wait(act, kvn_ready, s.n)
                nc.scalar.copy(g_sb[:], b_g[:, 0:D + 1]).then_inc(g_kept, 1)

            def keep_gt(s):
                act.wait_ge(g_turned, s.n + 1)
                nc.scalar.copy(gt_sb[:], b_g[:, GT0:GT0 + P]).then_inc(gt_kept, 1)

            def keep_ot(s, c):
                act.wait_ge(o_turned[c], s.n + 1)
                wait(act, y_made, (s.n - 1) * CH + (c + 1))
                nc.scalar.copy(ot[:, c, :], b_t[c][:]).then_inc(ot_ready[c], 1)

            def rough_root(s):
                act.wait_ge(var_ready, s.n + (AHEAD + 1))
                f(ln[:, s.u, 5, :], ln[:, s.u, 4, :], ACT.Ln).then_inc(log_ready, 1)
                act.wait_ge(log_ready, s.n + (AHEAD + 1))
                f(ln[:, s.u, 6, :], ln[:, s.u, 5, :], ACT.Exp, scale=-0.5).then_inc(root_ready, 1)

            def keep_x1t(s, c):
                act.wait_ge(x1_turned[c], s.n + 1)
                wait(act, logits_made, s.n)
                nc.scalar.copy(x1t[:, c, :], b_t[c][:]).then_inc(x1t_ready[c], 1)

            def payload(s, c):
                if c == 0:
                    act.wait_ge(ln_ready, s.n + (AHEAD + 1))
                    act.wait_ge(exps, s.n + 1)
                for j in range(c * TC, (c + 1) * TC):
                    ins = f(pay[:, s.u, j, 0:D], x1[:, s.u, j, :], ACT.Identity,
                            bias=ln[:, s.u, 9, j:j + 1], scale=ln[:, s.u, 8, j:j + 1])
                if c == CH - 1:
                    ins.then_inc(pay_x, 1)

            def exp_logits(s):
                wait(act, sent[s.u], s.half * (TILES * TOP * ON_QUEUE))
                act.wait_ge(shifted, s.n + 1)
                f(expo[:], expo[:], ACT.Exp).then_inc(exps, 1)

            def step(do, t):
                do(exp_k, 1, 0)
                do(payload, 3, 0)
                do(keep_xt, 1, 1)
                do(keep_ot, 2, 0)
                do(payload, 3, 1)
                do(exp_q, 1, 0)
                do(keep_ot, 2, 1)
                do(exp_k, 1, 1)
                do(exp_q, 1, 1)
                do(keep_g, 1)
                do(keep_x1t, 2, 0)
                do(rough_root, 2, first=-AHEAD)
                do(keep_gt, 1)
                do(keep_x1t, 2, 1)
                do(first_norm, 0, 0)
                do(exp_logits, 2)
                do(keep_xt, 0, 0)
                do(first_norm, 0, 1)

            nc.scalar.preload_act_table_set("natural_log_exp_and_others")
            act.wait_ge(filled, 1)
            run(act, step, 0, NB + 2, (4, 8))

            def split_weights(e):
                wait(act, e_made, (e.n - 1) * NCH)
                act.wait_ge(w1_in[e.u], (e.half + 1) * ON_QUEUE)
                act.wait_ge(w2_in[e.u], (e.half + 1) * ON_QUEUE)
                nc.scalar.copy(w1_hl[0][:, e.u], w1[:, e.u])
                nc.scalar.copy(w2_hl[0][:, e.u].rearrange("p i d -> p (i d)"),
                               w2[:, e.u].rearrange("p i d -> p (i d)")).then_inc(w_hi_ready, 1)

            def split_rows(e, m):
                c, v = chunk(e, m)
                act.wait_ge(r_turned, c + 1)
                wait(act, h_made, c * 2 - 2)
                nc.scalar.copy(rt_hl[0][:, v, :], bank[v][:, 0:PAIR * P]).then_inc(rt_hi_ready, 1)

            def relu(e, m):
                c, v = chunk(e, m)
                for h in range(2):
                    act.wait_ge(h_made, c * 2 + h + 1)
                    if h == 0:
                        wait(act, e_made, c - 1)
                    f(hid_hl[0][:, v, 2 * h:2 * h + 2, :].rearrange("p i n -> p (i n)"), bank[2 + 2 * v + h][:],
                      ACT.Relu).then_inc(h_hi_ready, 1)

            def keep_yt(e, m):
                c, v = chunk(e, m)
                act.wait_ge(e_made, c + 1)
                wait(act, y_turned, c - 1)
                nc.scalar.copy(yt[:, v, :], bank[6 + v][:, 0:PAIR * P]).then_inc(yt_ready, 1)

            run_experts(act, lambda before, e, after: walk(
                before, e, after, split_weights, split_rows, relu, keep_yt, lambda e, m: None))

        @block.vector
        def _(dve):
            v = nc.vector
            v.memset(empty[:], 0.0).then_inc(empty_set, 1)
            dve.wait_ge(empty_set, 1)
            v.memset(empty[:, :, D + E].bitcast(I32), NB * S).then_inc(empty_set, 1)
            v.memset(xn[:, :, :, D:D + 1], 1.0)
            v.memset(seen[:], 0.0)
            v.memset(stats[:], 0.0)
            v.memset(minus_one[:], -1.0)
            v.memset(taken[:], 0.0).then_inc(filled, 1)
            spread_links = Chain(dve, spread_chain, 3, -AHEAD)
            newton_links = Chain(dve, newton_chain, 3, -AHEAD)
            o_links, choose_links, weigh_links, place_links = (
                Chain(dve, c, n) for c, n in ((o_chain, 4 * CH), (choose_chain, 4), (weigh_chain, 4), (place_chain, 4)))

            def first_stats(t):
                for s in (Seq.fixed(2 * t), Seq.fixed(2 * t + 1)):
                    dve.wait_ge(x_in[s.u], (s.half + 1) * ON_QUEUE)
                    for k in range(TILES):
                        ins = v.bn_stats(stats[:, s.n, TILES + k, :], xs[:, s.n, k, :])
                    ins.then_inc(stats1_ready, 1)

            def spread(s):
                wait(dve, xn_ready, (s.n + 1) * CH)
                wait(dve, pay_x, s.n - 1)
                dve.wait_ge(stats1_ready, min(s.n + (AHEAD + 1), NB) if isinstance(s.n, int) else NB)
                wait(dve, stats2_ready, s.n + 1)
                r, st, ch = ln[:, s.u], stats[:, s.n + AHEAD], spread_links
                ch.begin(s)
                v.tensor_tensor(r[:, 3, :], st[:, :, 2], st[:, :, 5], ALU.add)
                halves = ch.tick(v.tensor_tensor(r[:, 1, :], st[:, :, 1], st[:, :, 4], ALU.subtract))
                v.tensor_tensor(r[:, 0, :], st[:, :, 1], st[:, :, 4], ALU.add)
                ch.after(halves)
                ch.link(v.tensor_tensor(r[:, 1, :], r[:, 1, :], r[:, 1, :], ALU.mult))
                ch.link(v.scalar_tensor_tensor(out=r[:, 3, :], in0=r[:, 1, :], scalar=D / 4.0, in1=r[:, 3, :],
                                               op0=ALU.mult, op1=ALU.add))
                ch.end()
                v.tensor_scalar(r[:, 4, :], r[:, 3, :], 1.0 / D, LN_EPS, ALU.mult, ALU.add).then_inc(var_ready, 1)

            def newton(s):
                dve.wait_ge(root_ready, s.n + (AHEAD + 1))
                r, ch = ln[:, s.u], newton_links
                ch.begin(s)
                ch.link(v.tensor_tensor(r[:, 7, :], r[:, 6, :], r[:, 6, :], ALU.mult))
                ch.link(v.scalar_tensor_tensor(out=r[:, 7, :], in0=r[:, 7, :], scalar=-0.5, in1=r[:, 4, :],
                                               op0=ALU.mult, op1=ALU.mult))
                ch.link(v.scalar_tensor_tensor(out=r[:, 8, :], in0=r[:, 7, :], scalar=1.5, in1=r[:, 6, :],
                                               op0=ALU.add, op1=ALU.mult))
                ch.end()
                v.scalar_tensor_tensor(out=r[:, 9, :], in0=r[:, 0, :], scalar=-0.5, in1=r[:, 8, :],
                                       op0=ALU.mult, op1=ALU.mult).then_inc(ln_ready, 1)

            def phi_k(s, c):
                dve.wait_ge(k_exp, s.n * CH + (c + 1))
                wait(dve, g_made if c else g_half, s.n)
                v.scalar_tensor_tensor(out=phik[:, c, :], in0=b_k[:], scalar=1.0, in1=kx[:, c, :],
                                       op0=ALU.max, op1=ALU.min).then_inc(phik_ready, 1)

            def phi_q(s, c):
                dve.wait_ge(q_exp, s.n * CH + (c + 1))
                wait(dve, o_made, (s.n - 1) * CH)
                v.scalar_tensor_tensor(out=phiqt[:, s.u, c, :], in0=b_q[:], scalar=1.0, in1=qx[:, c, :],
                                       op0=ALU.max, op1=ALU.min).then_inc(phiq_ready, 1)

            def mask_kv(s):
                dve.wait_ge(kv_made, s.n + 1)
                wait(dve, o_made, s.n * CH)
                v.tensor_tensor(kvn[:, 0:D], b_g[:, KV0:KV0 + P], head_mask[:].rearrange("p h j -> p (h j)"),
                                ALU.mult)
                v.tensor_scalar(kvn[:, D:ON], head_sel[:], g_sb[:, D:D + 1], None, ALU.mult).then_inc(kvn_ready, 1)

            def normalise_o(s, c):
                dve.wait_ge(o_made, s.n * CH + (c + 1))
                wait(dve, o_turned[c], s.n)
                ch = o_links
                ch.begin(s, done=c * ch.per // CH)
                def heads(h):
                    return slice(h * 2 * HEADS, (h + 1) * 2 * HEADS)

                floored = [ch.tick(v.tensor_scalar(
                    nrm[:, c, heads(h)].rearrange("p (k n) -> p k n", k=2),
                    o_bank[h][:].rearrange("p (k n) -> p k n", n=256)[:, :, D:ON], NORM_MIN, None, ALU.max))
                    for h in range(2)]
                inverse = []
                for h in range(2):
                    ch.after(floored[h])
                    inverse.append(ch.tick(v.reciprocal(rnrm[:, c, heads(h)], nrm[:, c, heads(h)])))
                for h in range(2):
                    ch.after(inverse[h])
                    src = o_bank[h][:].rearrange("p (k n) -> p k n", n=256)[:, :, 0:D]
                    r = rnrm[:, c, heads(h)].rearrange("p (k h a) -> p k h a", k=2, a=1)
                    ins = v.tensor_tensor(
                        on[:, c, h * 256:(h + 1) * 256].rearrange("p (k h j) -> p k h j", k=2, j=HD),
                        src.rearrange("p k (h j) -> p k h j", j=HD), r.to_broadcast([P, 2, HEADS, HD]), ALU.mult)
                ins.then_inc(o_ready, 1)

            def residual(s, c):
                dve.wait_ge(y_made, s.n * CH + (c + 1))
                if c == 0:
                    wait(dve, x1_stored[s.u], s.half * ON_QUEUE)
                    wait(dve, pay_x, s.n - 1)
                    wait(dve, x1_turned[1], s.n - 1)
                half = x1[:, s.u, c * TC:(c + 1) * TC, :]
                v.tensor_tensor(half, b_y[:].rearrange("p (t d) -> p t d", d=D),
                                xs[:, s.n, c * TC:(c + 1) * TC, :], ALU.add).then_inc(x1_ready, 1)
                dve.wait_ge(x1_ready, s.n * CH + (c + 1))
                for k in range(TC):
                    ins = v.bn_stats(stats[:, s.n + AHEAD, c * TC + k, :], half[:, k, :])
                if c == CH - 1:
                    ins.then_inc(stats2_ready, 1)

            def bcast_e(m):
                return m[:].rearrange("p (a e) -> p a e", a=1).to_broadcast([P, TILES, E])

            def wide(m):
                return m.rearrange("p (t a) -> p t a", a=1).to_broadcast([P, TILES, E])

            def choose(s):
                dve.wait_ge(logits_made, s.n + 1)
                dve.wait_ge(ln_ready, s.n + (AHEAD + 1))
                ch = choose_links
                ch.begin(s)
                v.tensor_tensor(logit[:], b_y[:, 0:TILES * E].rearrange("p (t e) -> p t e", e=E),
                                wide(ln[:, s.u, 8, 0:TILES]), ALU.mult).then_inc(logits_kept, 1)
                dve.wait_ge(logits_kept, s.n + 1)
                ch.link(v.tensor_tensor(logit[:], logit[:], bcast_e(bias_e), ALU.add))
                v.tensor_tensor(seen[:], seen[:], taken[:], ALU.add)
                for k in range(TILES):
                    ins = v.max(top_val[:, k, :], logit[:, k, :])
                ch.link(ins)
                v.tensor_tensor(expo[:], logit[:], top_val[:, :, 0:1].to_broadcast([P, TILES, E]),
                                ALU.subtract).then_inc(shifted, 1)
                for k in range(TILES):
                    ins = v.max_index(top_idx[:, k, :], top_val[:, k, :], logit[:, k, :])
                ch.link(ins)
                ch.link(v.tensor_tensor(
                    chosen[:], number_e[:].rearrange("p (a t) e -> p a t e", a=1).to_broadcast([P, TOP, TILES, E]),
                    top_idx[:, :, 0:TOP].rearrange("p t (k a) -> p k t a", a=1).to_broadcast([P, TOP, TILES, E]),
                    ALU.is_equal))
                ch.end()
                v.tensor_tensor(either[:], chosen[:, 0], chosen[:, 1], ALU.add)

            def weigh(s):
                dve.wait_ge(exps, s.n + 1)
                weight, number = pay[:, s.u, :, D:D + E], pay[:, s.u, :, D + E].bitcast(I32)
                ch = weigh_links
                ch.begin(s)
                summed = ch.tick(v.tensor_reduce(total[:, 0, :], expo[:], AX.X, ALU.add))
                v.tensor_scalar(number, number, 2 * S, None, ALU.add)
                ch.after(summed)
                ch.link(v.reciprocal(total[:, 1, :], total[:, 0, :]))
                ch.link(v.tensor_tensor(weight, expo[:], wide(total[:, 1, :]), ALU.mult))
                wait(dve, pos_made, s.n)
                v.scalar_tensor_tensor(out=mask_bf[:], in0=weight, scalar=0.0, in1=either[:],
                                       op0=ALU.is_gt, op1=ALU.mult).then_inc(mask_ready, 1)
                dve.wait_ge(mask_ready, s.n + 1)
                ch.link(v.scalar_tensor_tensor(out=base_m[:], in0=mask_bf[:], scalar=-FAR, in1=base_e[:],
                                               op0=ALU.mult, op1=ALU.add))
                ch.end()

            def find_places(s):
                dve.wait_ge(pos_made, s.n + 1)
                ch = place_links
                ch.begin(s)
                pos = b_y[:, POS0:2 * POS0].rearrange("p (t e) -> p t e", e=E)
                ch.tick(v.tensor_scalar(over[:], pos, float(CAP), FAR, ALU.is_ge, ALU.mult))
                v.tensor_tensor(place[:], pos, base_m[:], ALU.add).then_inc(places_read, 1)
                dve.wait_ge(places_read, s.n + 1)
                moved = ch.tick(v.tensor_tensor(place[:], place[:], over[:], ALU.add))
                v.tensor_reduce(taken[:], mask_bf[:].rearrange("p t e -> p e t"), AX.X, ALU.add)
                ch.after(moved)
                ch.link(v.tensor_tensor(
                    place_k[:].rearrange("p k t e -> p k (t e)"), chosen[:].rearrange("p k t e -> p k (t e)"),
                    place[:].rearrange("p (a t) e -> p a (t e)", a=1).to_broadcast([P, TOP, TILES * E]), ALU.mult))
                ch.link(v.tensor_reduce(choice[:], place_k[:], AX.X, ALU.add))
                ch.end()
                v.tensor_copy(spot[:, s.u], choice[:]).then_inc(spots_ready, 1)

            def step(do, t):
                do(mask_kv, 1)
                do(choose, 2)
                do(normalise_o, 1, 0)
                do(weigh, 2)
                if t <= 2:
                    first_stats(t + 1)
                do(phi_k, 0, 0)
                do(find_places, 2)
                do(normalise_o, 1, 1)
                do(residual, 1, 0)
                do(phi_q, 0, 0)
                do(phi_k, 0, 1)
                do(residual, 1, 1)
                do(spread, 1, first=-AHEAD)
                do(phi_q, 0, 1)
                do(newton, 1, first=-AHEAD)

            dve.wait_ge(w_turned, 1)
            v.tensor_copy(w_t[:].rearrange("p c d -> p (c d)"), b_t0[:])
            v.tensor_copy(wr_raw_t[:], b_t1[:, 0:E])
            dve.wait_ge(const_done, 8)
            dve.wait_ge(wr_in, ON_QUEUE)
            dve.wait_ge(payload_ids, 2)
            dve.wait_ge(filled, 1)
            v.tensor_copy(ident_bf[:], ident[:]).then_inc(w_kept, 1)
            dve.wait_ge(wr_summed, 1)
            v.scalar_tensor_tensor(out=wr_t[:], in0=b_y[:, 0:E], scalar=-1.0 / D, in1=wr_raw_t[:],
                                   op0=ALU.mult, op1=ALU.add).then_inc(wr_centred, 1)
            run(dve, step, -1, NB + 1, (4, 8))

            def low(out, x, hi):
                return v.tensor_tensor(out, x, hi.bitcast(F32), ALU.subtract)

            def split_weights(e):
                dve.wait_ge(w_hi_ready, e.n + 1)
                low(w1_hl[1][:, e.u], w1[:, e.u], w1_hl[0][:, e.u])
                low(w2_hl[1][:, e.u], w2[:, e.u], w2_hl[0][:, e.u]).then_inc(w_lo_ready, 1)

            def split_rows(e, m):
                c, w = chunk(e, m)
                dve.wait_ge(rt_hi_ready, c + 1)
                low(rt_hl[1][:, w, :], bank[w][:, 0:PAIR * P], rt_hl[0][:, w, :]).then_inc(rt_lo_ready, 1)

            def relu(e, m):
                c, w = chunk(e, m)
                for h in range(2):
                    dve.wait_ge(h_hi_ready, c * 2 + h + 1)
                    hi, lo = (x[:, w, 2 * h:2 * h + 2, :].rearrange("p i n -> p (i n)") for x in hid_hl)
                    v.scalar_tensor_tensor(out=lo, in0=bank[2 + 2 * w + h][:], scalar=0.0, in1=hi.bitcast(F32),
                                           op0=ALU.max, op1=ALU.subtract).then_inc(h_lo_ready, 1)

            def keep_tags(e, m):
                if m == 0:
                    dve.wait_ge(first_rows_in[e.u], (e.half + 1) * ON_QUEUE)
                    dve.wait_ge(rows_in[e.u], (e.half + 1) * ON_QUEUE)
                    wait(dve, added[e.u], e.half * (ET * ON_QUEUE))
                    v.tensor_copy(row_weights[:, e.u], rows[:, e.u, :, D:D + E])
                    v.tensor_copy(row_tokens[:, e.u], rows[:, e.u, :, D + E].bitcast(I32)).then_inc(tags_kept, 1)

            def weigh_out(e, m):
                c, w = chunk(e, m)
                dve.wait_ge(y_turned, c + 1)
                if m == 0:
                    dve.wait_ge(tags_kept, e.n + 1)
                for k in range(PAIR):
                    j = m * PAIR + k
                    ins = v.tensor_scalar(yo[:, e.u, j, :], bank[6 + w][:, 256 + k * P:256 + (k + 1) * P],
                                          row_weights[:, e.u, j, bass.ds(e.n, 1)], None, ALU.mult)
                ins.then_inc(yo_ready, 1)

            run_experts(dve, lambda before, e, after: walk(
                before, e, after, split_weights, split_rows, relu, keep_tags, weigh_out))


_INS = ["L0_attn_x", "L0_attn_w_qkv", "L0_attn_w_out", "L0_ffn_W_router", "L0_ffn_b_router",
        "L0_ffn_experts_inter", "L0_ffn_experts_out"]
_OUTS = [((8, 1024, 128), "float32")]


def kernel(**inputs):
    import numpy as _np
    import concourse.bacc as _bacc
    from concourse import mybir as _mybir
    from concourse.bass_utils import run_bass_kernel_spmd as _run

    nc = _bacc.Bacc("TRN2", target_bir_lowering=False, num_devices=1)
    arrays, args = {}, []
    for name in _INS:
        a = _np.ascontiguousarray(inputs[name])
        arrays[f"in_{name}_dram"] = a
        args.append(nc.dram_tensor(f"in_{name}_dram", a.shape, _mybir.dt.from_np(a.dtype), kind="ExternalInput").ap())
    for i, (shape, dtype) in enumerate(_OUTS):
        dt = _mybir.dt.from_np(_np.dtype(dtype))
        args.append(nc.dram_tensor(f"out_{i}_dram", shape, dt, kind="ExternalOutput").ap())
    moe_layer(nc, *args)
    r = _run(nc, [arrays], core_ids=[0])
    got = tuple(r.results[0][f"out_{i}_dram"] for i in range(len(_OUTS)))
    return got[0]
```
